# Optimizing a Trainium2 kernel written in Bass

```python
import numpy as np
import jax
import jax.numpy as jnp

def _softmax(x, axis=-1):
    return jax.nn.softmax(x, axis=axis)

def _gelu(x):
    return jax.nn.gelu(x, approximate=True)

def _silu(x):
    return jax.nn.silu(x)

def _sigmoid(x):
    return jax.nn.sigmoid(x)

def _layernorm(x, axis=-1, eps=1e-05):
    m = jnp.mean(x, axis=axis, keepdims=True)
    v = jnp.var(x, axis=axis, keepdims=True)
    return (x - m) / jnp.sqrt(v + eps)

def _scatter_add(tgt, idx, src, axis=0):
    return tgt.at[idx].add(src)

def _segment_sum(src, seg, n):
    return jax.ops.segment_sum(src, seg, n)
kernel_name = 'mk_seq_preln_d1_jaxref_r8_93ebb0'

def setup_inputs(seed: int=0):
    np.random.seed(seed)
    _w = jnp.asarray

    def _L0_attn_setup():
        import jax, jax.numpy as jnp
        import numpy as np
        from jax import lax
        N_EMBD = 128
        N_HEAD = 16
        HEAD_DIM = N_EMBD // N_HEAD
        EPS = 1e-06
        B, T = (4, 256)

        def _feature_map(x):
            return jax.nn.elu(x) + 1.0
        key = jax.random.key(seed)
        ks = jax.random.split(key, 5)
        scale = 1.0 / np.sqrt(N_EMBD)
        return {'x': jax.random.normal(ks[0], (B, T, N_EMBD), jnp.float32), 'W_attn': jax.random.normal(ks[1], (N_EMBD, 3 * N_EMBD), jnp.float32) * scale, 'b_attn': jax.random.normal(ks[2], (3 * N_EMBD,), jnp.float32) * 0.01, 'W_proj': jax.random.normal(ks[3], (N_EMBD, N_EMBD), jnp.float32) * scale, 'b_proj': jax.random.normal(ks[4], (N_EMBD,), jnp.float32) * 0.01}
    _L0_attn_in = _L0_attn_setup()

    def _L0_ffn_setup():
        import jax, jax.numpy as jnp
        import numpy as np
        B, S, D = (4, 256, 128)
        EXP = 4
        H = EXP * D
        E = 8
        TOP_K = 2
        key = jax.random.key(seed)
        ks = jax.random.split(key, 8)
        scale1 = 1.0 / np.sqrt(D)
        scale2 = 1.0 / np.sqrt(H)
        x = jax.random.normal(ks[0], (B, S, D), dtype=jnp.float32)
        W1 = jax.random.uniform(ks[1], (E, D, H), jnp.float32, -scale1, scale1)
        b1 = jax.random.uniform(ks[2], (E, H), jnp.float32, -scale1, scale1)
        W2 = jax.random.uniform(ks[3], (E, H, D), jnp.float32, -scale2, scale2)
        b2 = jax.random.uniform(ks[4], (E, D), jnp.float32, -scale2, scale2)
        Wr = jax.random.uniform(ks[5], (D, E), jnp.float32, -scale1, scale1)
        br = jax.random.uniform(ks[6], (E,), jnp.float32, -scale1, scale1)
        return {'input_emb': x, 'W1': W1, 'b1': b1, 'W2': W2, 'b2': b2, 'Wr': Wr, 'br': br}
    _L0_ffn_in = _L0_ffn_setup()
    _d = {'L0_attn_x': _L0_attn_in['x'], 'L0_attn_W_attn': _L0_attn_in['W_attn'], 'L0_attn_b_attn': _L0_attn_in['b_attn'], 'L0_attn_W_proj': _L0_attn_in['W_proj'], 'L0_attn_b_proj': _L0_attn_in['b_proj'], 'L0_ffn_W1': _L0_ffn_in['W1'], 'L0_ffn_b1': _L0_ffn_in['b1'], 'L0_ffn_W2': _L0_ffn_in['W2'], 'L0_ffn_b2': _L0_ffn_in['b2'], 'L0_ffn_Wr': _L0_ffn_in['Wr'], 'L0_ffn_br': _L0_ffn_in['br']}
    _x0 = _d['L0_attn_x']
    _d['L0_attn_x'] = jax.random.normal(jax.random.fold_in(jax.random.key(seed), 1), (16, 256, 128), dtype=_x0.dtype)
    del _x0
    return _d

def reference(L0_attn_x, L0_attn_W_attn, L0_attn_b_attn, L0_attn_W_proj, L0_attn_b_proj, L0_ffn_W1, L0_ffn_b1, L0_ffn_W2, L0_ffn_b2, L0_ffn_Wr, L0_ffn_br):

    def _L0_attn_ref(x, W_attn, b_attn, W_proj, b_proj):
        import jax, jax.numpy as jnp
        import numpy as np
        from jax import lax
        N_EMBD = 128
        N_HEAD = 16
        HEAD_DIM = N_EMBD // N_HEAD
        EPS = 1e-06
        B, T = (4, 256)

        def _feature_map(x):
            return jax.nn.elu(x) + 1.0
        Bb, Tt, C = x.shape
        qkv = x @ W_attn + b_attn
        q, k, v = jnp.split(qkv, 3, axis=-1)

        def to_heads(t):
            return t.reshape(Bb, Tt, N_HEAD, HEAD_DIM).transpose(1, 0, 2, 3)
        q = _feature_map(to_heads(q))
        k = _feature_map(to_heads(k))
        v = to_heads(v)

        def step(carry, inp):
            kv, ksum = carry
            qt, kt, vt = inp
            kv = kv + kt[..., :, None] * vt[..., None, :]
            ksum = ksum + kt
            num = jnp.einsum('bhi,bhij->bhj', qt, kv)
            den = jnp.einsum('bhi,bhi->bh', qt, ksum)[..., None] + EPS
            return ((kv, ksum), num / den)
        init = (jnp.zeros((Bb, N_HEAD, HEAD_DIM, HEAD_DIM), x.dtype), jnp.zeros((Bb, N_HEAD, HEAD_DIM), x.dtype))
        _, y = lax.scan(step, init, (q, k, v))
        y = y.transpose(1, 0, 2, 3).reshape(Bb, Tt, C)
        return y @ W_proj + b_proj

    def _L0_ffn_ref(input_emb, W1, b1, W2, b2, Wr, br):
        import jax, jax.numpy as jnp
        import numpy as np
        B, S, D = (4, 256, 128)
        EXP = 4
        H = EXP * D
        E = 8
        TOP_K = 2
        logits = jnp.einsum('bsd,de->bse', input_emb, Wr) + br
        route_w = jax.nn.softmax(logits, axis=-1)
        _, topk_idx = jax.lax.top_k(route_w, TOP_K)
        mask = jax.nn.one_hot(topk_idx, E, dtype=route_w.dtype).sum(-2)
        routed = route_w * mask
        routed = routed / routed.sum(axis=-1, keepdims=True)
        h = jax.nn.relu(jnp.einsum('bsd,edh->ebsh', input_emb, W1) + b1[:, None, None, :])
        expert_out = jnp.einsum('ebsh,ehd->ebsd', h, W2) + b2[:, None, None, :]
        return jnp.einsum('bse,ebsd->bsd', routed, expert_out)
    x = L0_attn_x
    x = x + _L0_attn_ref(_layernorm(x, axis=-1), L0_attn_W_attn, L0_attn_b_attn, L0_attn_W_proj, L0_attn_b_proj)
    x = x + _L0_ffn_ref(_layernorm(x, axis=-1), L0_ffn_W1, L0_ffn_b1, L0_ffn_W2, L0_ffn_b2, L0_ffn_Wr, L0_ffn_br)
    return x

_drawn_inputs = setup_inputs


def setup_inputs(seed=0):
    import zlib

    import numpy as np

    out = dict(_drawn_inputs(seed))
    spreads = {}
    factors = {'L0_attn_b_attn': 3.594, 'L0_attn_b_proj': 3.761, 'L0_ffn_b1': 3.826, 'L0_ffn_b2': 3.225}
    for name, (base, spread) in spreads.items():
        noise = np.random.default_rng([zlib.crc32(name.encode()), seed]).standard_normal(out[name].shape)
        drawn = base * np.exp(spread * noise) if base else spread * noise
        out[name] = jnp.asarray(drawn.astype(out[name].dtype))
    for name, factor in factors.items():
        out[name] = (out[name] * factor).astype(out[name].dtype)
    return out
```

```python
from contextlib import ExitStack

import concourse.bass as bass
from concourse import mybir

F32 = mybir.dt.float32
F16 = mybir.dt.float16
BF16 = mybir.dt.bfloat16
I32 = mybir.dt.int32
ALU = mybir.AluOpType
ACT = mybir.ActivationFunctionType
AX = mybir.AxisListType


def block_kernel(nc, x_d, wqkv_d, bqkv_d, wproj_d, bproj_d, w1_d, b1_d, w2_d, b2_d, wr_d, br_d, out_d):
    P = 128
    SEQS, T, D = x_d.shape
    NT = SEQS * T // P
    U = SEQS
    TPU = T // P
    H, DH = 16, D // 16
    E, _, HID = w1_d.shape
    HC = HID // P
    DV = DH + 1
    KV = DV * DH
    LN_EPS, DEN_EPS = 1e-5, 1e-6
    LOADS = 4
    TPL = NT // LOADS
    assert TPU == 2 and D == P and U % 2 == 0

    HEADS = [(0, 6), (6, 11), (11, 16)]
    X_SCALE = 2.0 ** 11
    W_TOP = 2.0 ** 9
    H_TOP = 2.0 ** 14
    TOK = 512
    NB = NT * P // TOK
    SUB = TOK // P

    xv = x_d.rearrange("s (a p) d -> p (s a) d", p=P)
    ov = out_d.rearrange("s (a p) d -> p (s a) d", p=P)

    with ExitStack() as ctx:
        def sb(name, shape, dt=F32):
            return ctx.enter_context(nc.sbuf_tensor(name, shape, dt))

        def sem(name):
            return ctx.enter_context(nc.semaphore(name))

        ps = ctx.enter_context(nc.psum_tensor("ps", [P, 8, 512], F32))

        x = sb("x", [P, NT, D])
        wqkv = sb("wqkv", [P, 3 * D])
        bqkv = sb("bqkv", [P, 3 * D])
        wproj = sb("wproj", [P, D])
        bproj = sb("bproj", [P, D])
        wr = sb("wr", [P, E])
        br = sb("br", [P, E])
        w1h = sb("w1h", [P, E, HID], F16)
        w1l = sb("w1l", [P, E, HID], F16)
        w2h = sb("w2h", [P, E, HC, D], F16)
        w2l = sb("w2l", [P, E, HC, D], F16)
        wf = sb("wf", [P, 2, E * HID])
        b1r = sb("b1r", [E * HC, P])
        b1T = sb("b1T", [P, E * HC])
        b1s = sb("b1s", [P, E * HC])
        b2p = sb("b2p", [3, E, D], BF16)
        ones3 = sb("ones3", [3, P], BF16)
        ident = sb("ident", [P, P])
        tri = sb("tri", [P, P])
        ones = sb("ones", [P, P])
        neghalf = sb("neghalf", [P, NT])
        iota_i = sb("iota_i", [P, E], I32)
        iota = sb("iota", [P, E])
        st = sb("st", [P, NT, 6])
        lnt = sb("lnt", [P, 7, NT])
        rstd = sb("rstd", [P, 2, NT])
        xn_s = sb("xn_s", [P, 2, TPU, D])
        xT_s = sb("xT_s", [P, 2, T])
        work = sb("work", [P, 2 * H * KV])
        qk = sb("qk", [P, NT, 2 * D])
        vaug = sb("vaug", [P, NT, H, DV])
        kv_s = sb("kv_s", [P, 2, TPU, H, KV])
        nd = sb("nd", [P, NT, H * DV])
        rd = sb("rd", [P, NT, H])
        lg = sb("lg", [P, NT, E])
        r8 = sb("r8", [P, 5, NT, E])
        r1 = sb("r1", [P, 8, NT])
        routed = sb("routed", [P, NT, E])
        b2hml = sb("b2hml", [1, 3, E * D], BF16)
        sc = sb("sc", [P, 24])
        ndf = nd[:, :, :].rearrange("p t n -> p (t n)")
        xTh = ndf[:, 0:NT * P // 2].bitcast(F16)
        xTl = ndf[:, NT * P // 2:NT * P].bitcast(F16)
        kvf = kv_s[:, :, :, :, :].rearrange("p b a h n -> p (b a h n)")
        b2r, b2s, b2f = (kvf[0:1, n * E * D:(n + 1) * E * D] for n in range(3))
        te = work[:, 0:4 * T * 2].rearrange("p (w a t d) -> p w a t d", w=2, a=2, t=TPU)
        t_s, e_s = te[:, 0], te[:, 1]
        m_s = work[:, :].rearrange("p (a n) -> p a n", a=2)
        h32 = qk[:, 0:16, :].rearrange("p (b c n) d -> p b c (n d)", b=2, c=HC)
        hh = vaug[:, 0:15, :, :].rearrange("p t h d -> p (t h d)")[:, 0:2048].bitcast(F16).rearrange(
            "p (b c n) -> p b c n", b=2, c=HC)
        hl = vaug[:, 15:31, :, :].rearrange("p t h d -> p (t h d)")[:, 0:2048].bitcast(F16).rearrange(
            "p (b c n) -> p b c n", b=2, c=HC)

        x_in = [sem(f"x_in{g}") for g in range(LOADS)]
        wq_in = sem("wq_in")
        w1_in = sem("w1_in")
        w2_in = sem("w2_in")
        small_in = [sem(f"small_in{g}") for g in range(7)]
        const_done = sem("const_done")
        chain = sem("chain")
        pchain = sem("pchain")
        achain = sem("achain")
        stats_done = sem("stats_done")
        rstd_done = sem("rstd_done")
        bn_done = sem("bn_done")
        norm_done = sem("norm_done")
        xT_done = sem("xT_done")
        xT_out = sem("xT_out")
        qkv_done = sem("qkv_done")
        qkv_free = sem("qkv_free")
        t_done = sem("t_done")
        relu_done = sem("relu_done")
        exp_done = sem("exp_done")
        phi_done = sem("phi_done")
        kv_done = sem("kv_done")
        pfx_done = sem("pfx_done")
        m_done = sem("m_done")
        red_done = sem("red_done")
        xb_done = sem("xb_done")
        y_done = sem("y_done")
        yT_done = sem("yT_done")
        yT_out = sem("yT_out")
        proj_done = sem("proj_done")
        x2_done = sem("x2_done")
        var2_done = sem("var2_done")
        norm2_done = sem("norm2_done")
        x2T_done = sem("x2T_done")
        x2T_out = sem("x2T_out")
        xh_done = sem("xh_done")
        xl_done = sem("xl_done")
        lg_done = sem("lg_done")
        lgs_done = sem("lgs_done")
        gap_done = sem("gap_done")
        gexp_done = sem("gexp_done")
        routed_done = sem("routed_done")
        b1T_done = sem("b1T_done")
        b1T_out = sem("b1T_out")
        wabs_done = sem("wabs_done")
        wmax_done = sem("wmax_done")
        wall_done = sem("wall_done")
        scale_done = sem("scale_done")
        whi_done = sem("whi_done")
        wlo_done = sem("wlo_done")
        b2_done = sem("b2_done")
        b2_in = sem("b2_in")
        up_done = sem("up_done")
        relu1_done = sem("relu1_done")
        hi_done = sem("hi_done")
        lo_done = sem("lo_done")
        down_done = sem("down_done")
        acc_done = sem("acc_done")
        out_done = sem("out_done")

        block = ctx.enter_context(nc.Block())

        def units(eng, body, first, end):
            with eng.Fori(first // 2, end // 2) as it:
                for par in range(2):
                    body(it * 2 + par, par)

        def tiles(t, u):
            return t[:, bass.ds(u * TPU, TPU)]

        @block.sync
        def _(sp):
            for g in range(LOADS):
                sp.dma_start(x[:, g * TPL:(g + 1) * TPL, :], xv[:, g * TPL:(g + 1) * TPL, :]).then_inc(x_in[g], 16)
            sp.dma_start(wf[:, 0, :].rearrange("p (e h) -> p e h", e=E), w1_d.rearrange("e d h -> d e h")).then_inc(w1_in, 16)
            sp.dma_start(wf[:, 1, :].rearrange("p (e c d) -> p e c d", e=E, c=HC),
                         w2_d.rearrange("e (c p) d -> p e c d", p=P)).then_inc(w2_in, 16)
            sp.wait_ge(pfx_done, NT + 2 * TPU)
            sp.dma_start(b2r, b2_d.rearrange("e d -> (e d)").unsqueeze(0)).then_inc(small_in[6], 16)
            sp.wait_ge(b2_done, 1)
            for r in range(3):
                sp.dma_start(b2p[r:r + 1, :, :].rearrange("p e d -> p (e d)"), b2hml[0:1, r, :]).then_inc(b2_in, 16)
            for b in range(NB):
                sp.wait_ge(acc_done, (b + 1) * E * SUB + 2 * SUB)
                sp.dma_start(ov[:, b * SUB:(b + 1) * SUB, :], x[:, b * SUB:(b + 1) * SUB, :]).then_inc(out_done, 16)
            sp.wait_ge(out_done, 16 * NB)

        @block.gpsimd
        def _(pool):
            nc.gpsimd.memset(ident[:], 0.0).then_inc(pchain, 1)
            nc.gpsimd.memset(ones[:], 1.0).then_inc(pchain, 1)
            nc.gpsimd.memset(ones3[:], 1.0).then_inc(const_done, 1)
            nc.gpsimd.memset(neghalf[:], -0.5).then_inc(const_done, 1)
            nc.gpsimd.memset(vaug[:, :, :, DH:DV], 1.0).then_inc(const_done, 1)
            nc.gpsimd.iota(iota_i[:], [[1, E]], base=0, channel_multiplier=0).then_inc(pchain, 1)
            pool.wait_ge(pchain, 3)
            nc.gpsimd.affine_select(out=ident[:], in_=ident[:], compare_op=ALU.not_equal, fill=1.0, base=0,
                                    pattern=[[-1, P]], channel_multiplier=1).then_inc(const_done, 1)
            nc.gpsimd.affine_select(out=tri[:], in_=ones[:], compare_op=ALU.is_ge, fill=0.0, base=0,
                                    pattern=[[1, P]], channel_multiplier=-1).then_inc(const_done, 1)
            nc.gpsimd.tensor_copy(iota[:], iota_i[:]).then_inc(const_done, 1)

            pool.wait_ge(const_done, 6)
            pool.wait_ge(stats_done, 1)
            nc.gpsimd.tensor_tensor(rstd[:, 0, :], lnt[:, 4, :], neghalf[:], ALU.pow).then_inc(rstd_done, 1)

            def kv_products(u, par):
                pool.wait_ge(phi_done, u + 3)
                pool.wait_ge(pfx_done, u * 2 + 2)
                for a in range(TPU):
                    k = qk[:, bass.ds(u * TPU + a, 1), D:2 * D].rearrange("p a (h i) -> p (a h) i", i=DH)
                    v = vaug[:, bass.ds(u * TPU + a, 1), :, :].rearrange("p a h j -> p (a h) j")
                    nc.gpsimd.tensor_tensor(kv_s[:, par, a].rearrange("p h (j i) -> p h j i", j=DV),
                                            k.unsqueeze(2).broadcast_to([P, H, DV, DH]),
                                            v.unsqueeze(3).broadcast_to([P, H, DV, DH]), ALU.mult).then_inc(kv_done, 1)

            units(pool, kv_products, 0, U // 2)
            pool.wait_ge(wmax_done, 3)
            nc.gpsimd.partition_all_reduce(sc[:, 4:7], sc[:, 0:3], P, bass.bass_isa.ReduceOp.max).then_inc(wall_done, 1)
            units(pool, kv_products, U // 2, U)
            pool.wait_ge(small_in[1], 16)
            for g in range(LOADS):
                xg = x[:, g * TPL:(g + 1) * TPL, :]
                nc.gpsimd.tensor_tensor(xg, xg, bproj[:, :].unsqueeze(1).broadcast_to([P, TPL, D]), ALU.add).then_inc(xb_done, 1)

            pool.wait_ge(var2_done, 1)
            nc.gpsimd.tensor_tensor(rstd[:, 1, :], lnt[:, 4, :], neghalf[:], ALU.pow).then_inc(rstd_done, 1)

        @block.scalar
        def _(act):
            act.dma_start(wqkv[:, :], wqkv_d).then_inc(wq_in, 16)
            act.dma_start(bqkv[:, :], bqkv_d.partition_broadcast(P)).then_inc(small_in[0], 16)
            act.dma_start(bproj[:, :], bproj_d.partition_broadcast(P)).then_inc(small_in[1], 16)
            act.dma_start(wproj[:, :], wproj_d).then_inc(small_in[2], 16)
            act.dma_start(wr[:, :], wr_d).then_inc(small_in[3], 16)
            act.dma_start(br[:, :], br_d.partition_broadcast(P)).then_inc(small_in[4], 16)
            act.dma_start(b1r[:, :], b1_d.rearrange("e (c p) -> (e c) p", p=P)).then_inc(small_in[5], 16)

            act.wait_ge(b1T_done, 1)
            nc.scalar.activation(b1T[:, :], ps[:, 6, 0:E * HC], ACT.Copy).then_inc(b1T_out, 1)
            act.wait_ge(b1T_out, 1)

            def copy_xT(u, par):
                act.wait_ge(xT_done, u + 1)
                nc.scalar.activation(xT_s[:, par, :], ps[:, par, 0:T], ACT.Copy).then_inc(xT_out, 1)

            copy_xT(0, 0)
            copy_xT(1, 1)

            def features(it, last):
                for par in range(2):
                    u = it * 2 + par
                    act.wait_ge(t_done, u + 1)
                    nc.scalar.activation(e_s[:, par], t_s[:, par], ACT.Relu, scale=-1.0).then_inc(relu_done, 1)
                    act.wait_ge(relu_done, u + 1)
                    nc.scalar.activation(e_s[:, par], e_s[:, par], ACT.Exp, scale=-1.0).then_inc(exp_done, 1)
                if not last:
                    for par in range(2):
                        copy_xT(it * 2 + par + 2, par)

            with act.Fori(0, U // 2 - 1) as it:
                features(it, False)
            features(U // 2 - 1, True)

            act.wait_ge(w1_in, 16)
            nc.scalar.activation(w1h[:].rearrange("p e h -> p (e h)").bitcast(BF16), wf[:, 0], ACT.Abs).then_inc(wabs_done, 1)
            act.wait_ge(w2_in, 16)
            nc.scalar.activation(w2h[:].rearrange("p e c d -> p (e c d)").bitcast(BF16), wf[:, 1], ACT.Abs).then_inc(wabs_done, 1)
            nc.scalar.activation(b1s[:], b1T[:], ACT.Abs).then_inc(wabs_done, 1)

            act.wait_ge(scale_done, 1)
            nc.scalar.activation(w1h[:].rearrange("p e h -> p (e h)"), wf[:, 0], ACT.Copy, scale=sc[:, 12:13]).then_inc(whi_done, 1)
            nc.scalar.activation(w2h[:].rearrange("p e c d -> p (e c d)"), wf[:, 1], ACT.Copy, scale=sc[:, 13:14]).then_inc(whi_done, 1)
            nc.scalar.activation(b1s[:], b1T[:], ACT.Copy, scale=sc[:, 17:18]).then_inc(achain, 1)

            def copy_yT(u, par):
                act.wait_ge(yT_done, u + 1)
                act.wait_ge(proj_done, u + 1)
                nc.scalar.activation(xT_s[:, par, :], ps[:, par, 0:T], ACT.Copy).then_inc(yT_out, 1)

            units(act, copy_yT, 0, U)

            def copy_x2T(u, par):
                act.wait_ge(x2T_done, u + 1)
                act.wait_ge(lg_done, u + 1)
                act.wait_ge(xl_done, u + 1)
                nc.scalar.activation(xT_s[:, par, :], ps[:, 4 + par, 0:T], ACT.Copy).then_inc(x2T_out, 1)
                nc.scalar.activation(xTh[:, bass.ds(u * T, T)], ps[:, 4 + par, 0:T], ACT.Copy, scale=X_SCALE).then_inc(xh_done, 1)

            units(act, copy_x2T, 0, U)

            act.wait_ge(gap_done, 1)
            nc.scalar.activation(r1[:, 4, :], r1[:, 3, :], ACT.Exp).then_inc(gexp_done, 1)

            act.wait_ge(achain, 1)

            def hidden(b, e):
                for c in range(HC):
                    n = b * (E * HC) + (e * HC + c)
                    act.wait_ge(up_done, n + 1)
                    act.wait_ge(lo_done, n + 1)
                    nc.scalar.activation(h32[:, e % 2, c], ps[:, c, :], ACT.Relu, bias=b1s[:, e * HC + c:e * HC + c + 1],
                                         scale=sc[:, 18:19]).then_inc(relu1_done, 1)
                    act.wait_ge(relu1_done, n + HC + 1)
                    act.wait_ge(down_done, b * E + (e + 1))
                    nc.scalar.activation(hh[:, e % 2, c], h32[:, e % 2, c], ACT.Copy).then_inc(hi_done, 1)

            with act.Fori(0, NB) as b:
                for e in range(E):
                    hidden(b, e)

        @block.vector
        def _(dve):
            count = {"chain": 0}

            def link(ins):
                count["chain"] += 1
                ins.then_inc(chain, 1)
                dve.wait_ge(chain, count["chain"])

            for s, n in ((qkv_free, 4), (phi_done, 2), (pfx_done, 2 * TPU), (m_done, 2), (red_done, 2), (proj_done, 2), (lg_done, 2),
                         (xl_done, 2), (x2_done, 2), (lgs_done, 2), (relu1_done, HC), (lo_done, 2 * HC), (down_done, 2),
                         (acc_done, 2 * SUB)):
                dve.sem_inc(s, n)

            for g in range(LOADS):
                dve.wait_ge(x_in[g], 16)
                with dve.Fori(0, TPL // 4) as i:
                    for j in range(4):
                        t = i * 4 + (j + g * TPL)
                        nc.vector.bn_stats(st[:, bass.ds(t, 1), :].rearrange("p a s -> p (a s)"),
                                           x[:, bass.ds(t, 1), :].rearrange("p a d -> p (a d)")).then_inc(bn_done, 1)
            dve.wait_ge(bn_done, NT)

            def moments():
                me, qe, mo, qo = (st[:, :, c] for c in (1, 2, 4, 5))
                nc.vector.tensor_tensor(lnt[:, 0, :], me, mo, ALU.add)
                link(nc.vector.tensor_tensor(lnt[:, 1, :], me, mo, ALU.subtract))
                nc.vector.tensor_tensor(lnt[:, 2, :], qe, qo, ALU.add)
                link(nc.vector.scalar_tensor_tensor(out=lnt[:, 5, :], in0=lnt[:, 1, :], scalar=0.25, in1=lnt[:, 1, :],
                                                    op0=ALU.mult, op1=ALU.mult))
                nc.vector.tensor_scalar(lnt[:, 3, :], lnt[:, 0, :], 0.5, None, ALU.mult)
                link(nc.vector.scalar_tensor_tensor(out=lnt[:, 6, :], in0=lnt[:, 2, :], scalar=1.0 / D, in1=lnt[:, 5, :],
                                                    op0=ALU.mult, op1=ALU.add))
                return nc.vector.tensor_scalar(lnt[:, 4, :], lnt[:, 6, :], LN_EPS, None, ALU.add)

            moments().then_inc(stats_done, 1)
            dve.wait_ge(stats_done, 1)
            dve.wait_ge(rstd_done, 1)

            def norm(u, par, which, done):
                for a in range(TPU):
                    t = u * TPU + a
                    ins = nc.vector.tensor_scalar(xn_s[:, par, a], x[:, bass.ds(t, 1), :].rearrange("p a d -> p (a d)"),
                                                  lnt[:, 3, bass.ds(t, 1)], rstd[:, which, bass.ds(t, 1)],
                                                  ALU.subtract, ALU.mult)
                ins.then_inc(done, 1)

            norm(0, 0, 0, norm_done)
            norm(1, 1, 0, norm_done)
            dve.wait_ge(small_in[0], 16)
            dve.wait_ge(const_done, 6)

            def project_in(it, last):
                for par in range(2):
                    u = it * 2 + par
                    pq = ps[:, 2 + 2 * par:4 + 2 * par, :]
                    dve.wait_ge(qkv_done, u + 1)
                    dve.wait_ge(phi_done, u + 1)
                    nc.vector.tensor_tensor(t_s[:, par], pq[:, :, 0:2 * D],
                                            bqkv[:, 0:2 * D].unsqueeze(1).broadcast_to([P, TPU, 2 * D]),
                                            ALU.add).then_inc(t_done, 1)
                    nc.vector.tensor_tensor(tiles(vaug, u)[:, :, :, 0:DH],
                                            pq[:, :, 2 * D:3 * D].rearrange("p a (h j) -> p a h j", j=DH),
                                            bqkv[:, 2 * D:3 * D].rearrange("p (h j) -> p h j", j=DH).unsqueeze(1)
                                            .broadcast_to([P, TPU, H, DH]), ALU.add).then_inc(qkv_free, 2)
                if not last:
                    for par in range(2):
                        norm(it * 2 + par + 2, par, 0, norm_done)
                for par in range(2):
                    u = it * 2 + par
                    dve.wait_ge(exp_done, u + 1)
                    nc.vector.scalar_tensor_tensor(out=tiles(qk, u), in0=t_s[:, par], scalar=0.0, in1=e_s[:, par],
                                                   op0=ALU.max, op1=ALU.add).then_inc(phi_done, 1)

            with dve.Fori(0, U // 2 - 1) as it:
                project_in(it, False)
            project_in(U // 2 - 1, True)

            for n, w in enumerate((w1h[:].rearrange("p e h -> p (e h)").bitcast(BF16),
                                   w2h[:].rearrange("p e c d -> p (e c d)").bitcast(BF16), b1s[:])):
                dve.wait_ge(wabs_done, n + 1)
                nc.vector.tensor_reduce(sc[:, n:n + 1], w, AX.X, ALU.max).then_inc(wmax_done, 1)

            def attend(u, par):
                for a in range(TPU):
                    t = u * TPU + a
                    dve.wait_ge(pfx_done, t + (2 * TPU + 1))
                    dve.wait_ge(red_done, t + 1)
                    q = qk[:, bass.ds(t, 1), 0:D].rearrange("p a (h i) -> p (a h) i", i=DH)
                    for g, (h0, h1) in enumerate(HEADS):
                        n = h1 - h0
                        ins = nc.vector.tensor_tensor(
                            m_s[:, a, h0 * KV:h1 * KV].rearrange("p (h j i) -> p h j i", j=DV, i=DH),
                            ps[:, 3 * a + g, 0:n * KV].rearrange("p (h j i) -> p h j i", j=DV, i=DH),
                            q[:, h0:h1, :].unsqueeze(2).broadcast_to([P, n, DV, DH]), ALU.mult)
                    ins.then_inc(m_done, 1)
                for a in range(TPU):
                    t = u * TPU + a
                    dve.wait_ge(m_done, t + 3)
                    nc.vector.tensor_reduce(nd[:, bass.ds(t, 1), :].rearrange("p a n -> p (a n)"),
                                            m_s[:, a].rearrange("p (n i) -> p n i", i=DH), AX.X, ALU.add).then_inc(red_done, 1)

            dve.wait_ge(phi_done, U + 2)
            units(dve, attend, 0, U)

            dve.wait_ge(wall_done, 1)
            i32 = lambda a, b: sc[:, a:b].bitcast(I32)
            EXPONENT = 0x7F800000
            link(nc.vector.tensor_scalar(sc[:, 8:10], sc[:, 4:6], 1e-18, None, ALU.max))
            link(nc.vector.tensor_scalar(i32(10, 12), i32(8, 10), EXPONENT, None, ALU.bitwise_and))
            link(nc.vector.reciprocal(sc[:, 8:10], sc[:, 10:12]))
            link(nc.vector.tensor_scalar(sc[:, 12:14], sc[:, 8:10], W_TOP, None, ALU.mult))
            link(nc.vector.scalar_tensor_tensor(out=sc[:, 14:15], in0=sc[:, 10:11], scalar=2.0 * D, in1=sc[:, 6:7],
                                                op0=ALU.mult, op1=ALU.add))
            link(nc.vector.tensor_scalar(i32(15, 16), i32(14, 15), EXPONENT, None, ALU.bitwise_and))
            link(nc.vector.reciprocal(sc[:, 16:17], sc[:, 15:16]))
            link(nc.vector.tensor_scalar(sc[:, 17:18], sc[:, 16:17], H_TOP, None, ALU.mult))
            nc.vector.scalar_tensor_tensor(out=sc[:, 18:19], in0=sc[:, 17:18], scalar=1.0 / (W_TOP * X_SCALE),
                                           in1=sc[:, 10:11], op0=ALU.mult, op1=ALU.mult)
            link(nc.vector.tensor_tensor(sc[:, 19:20], sc[:, 17:18], sc[:, 13:14], ALU.mult))
            nc.vector.reciprocal(sc[:, 20:21], sc[:, 19:20]).then_inc(scale_done, 1)

            dve.wait_ge(red_done, NT + 2)
            ndv = nd[:, :, :].rearrange("p t (h j) -> p t h j", j=DV)
            link(nc.vector.tensor_scalar(rd[:, :, :], ndv[:, :, :, DH], DEN_EPS, None, ALU.add))
            link(nc.vector.reciprocal(rd[:, :, :], rd[:, :, :]))
            dve.wait_ge(xb_done, LOADS)

            def quotient(u, par):
                nc.vector.tensor_tensor(xn_s[:, par].rearrange("p a (h j) -> p a h j", j=DH),
                                        tiles(ndv, u)[:, :, :, 0:DH],
                                        tiles(rd, u).unsqueeze(3).broadcast_to([P, TPU, H, DH]), ALU.mult).then_inc(y_done, 1)

            quotient(0, 0)
            quotient(1, 1)

            def residual(it, last):
                for par in range(2):
                    u = it * 2 + par
                    dve.wait_ge(proj_done, u + 3)
                    nc.vector.tensor_tensor(tiles(x, u), ps[:, 2 + par, 0:T].rearrange("p (a d) -> p a d", a=TPU), tiles(x, u),
                                            ALU.add).then_inc(x2_done, 1)
                if not last:
                    for par in range(2):
                        quotient(it * 2 + par + 2, par)
                for par in range(2):
                    u = it * 2 + par
                    dve.wait_ge(x2_done, u + 3)
                    for a in range(TPU):
                        nc.vector.bn_stats(st[:, bass.ds(u * TPU + a, 1), :].rearrange("p a s -> p (a s)"),
                                           x[:, bass.ds(u * TPU + a, 1), :].rearrange("p a d -> p (a d)")).then_inc(bn_done, 1)

            with dve.Fori(0, U // 2 - 1) as it:
                residual(it, False)
            residual(U // 2 - 1, True)
            dve.wait_ge(bn_done, 2 * NT)
            moments().then_inc(var2_done, 1)
            dve.wait_ge(var2_done, 1)

            dve.wait_ge(small_in[6], 16)
            link(nc.vector.tensor_scalar(b2s, b2r, sc[0:1, 19:20], None, ALU.mult))
            link(nc.vector.tensor_copy(b2hml[:, 0], b2s))
            link(nc.vector.tensor_tensor(b2f, b2s, b2hml[:, 0], ALU.subtract))
            link(nc.vector.tensor_copy(b2hml[:, 1], b2f))
            nc.vector.tensor_tensor(b2hml[:, 2], b2f, b2hml[:, 1], ALU.subtract).then_inc(b2_done, 1)
            dve.wait_ge(b2_done, 1)

            dve.wait_ge(rstd_done, 2)
            norm(0, 0, 1, norm2_done)
            norm(1, 1, 1, norm2_done)
            dve.wait_ge(small_in[4], 16)

            def route(it, last):
                for par in range(2):
                    u = it * 2 + par
                    dve.wait_ge(x2T_out, u + 1)
                    dve.wait_ge(xh_done, u + 1)
                    nc.vector.scalar_tensor_tensor(out=xTl[:, bass.ds(u * T, T)], in0=xT_s[:, par], scalar=X_SCALE,
                                                   in1=xTh[:, bass.ds(u * T, T)], op0=ALU.mult,
                                                   op1=ALU.subtract).then_inc(xl_done, 1)
                if not last:
                    for par in range(2):
                        norm(it * 2 + par + 2, par, 1, norm2_done)
                for par in range(2):
                    u = it * 2 + par
                    dve.wait_ge(lg_done, u + 3)
                    nc.vector.tensor_tensor(tiles(lg, u), ps[:, 6 + par, 0:TPU * E].rearrange("p (a e) -> p a e", a=TPU),
                                            br[:, :].unsqueeze(1).broadcast_to([P, TPU, E]), ALU.add).then_inc(lgs_done, 1)

            with dve.Fori(0, U // 2 - 1) as it:
                route(it, False)
            route(U // 2 - 1, True)

            dve.wait_ge(lgs_done, U + 2)
            over_e = lambda a: a.unsqueeze(2).broadcast_to([P, NT, E])
            iota_t = iota[:, :].unsqueeze(1).broadcast_to([P, NT, E])

            def top(values, best, where, scratch, onehot):
                link(nc.vector.tensor_reduce(best, values, AX.X, ALU.max))
                link(nc.vector.tensor_tensor(scratch, values, over_e(best), ALU.is_equal))
                link(nc.vector.scalar_tensor_tensor(out=onehot, in0=iota_t, scalar=-float(E), in1=scratch,
                                                    op0=ALU.add, op1=ALU.mult))
                link(nc.vector.tensor_reduce(where, onehot, AX.X, ALU.min))
                link(nc.vector.tensor_scalar(where, where, float(E), None, ALU.add))
                link(nc.vector.tensor_tensor(onehot, iota_t, over_e(where), ALU.is_equal))

            top(lg[:, :, :], r1[:, 0, :], r1[:, 5, :], r8[:, 0], r8[:, 1])
            link(nc.vector.tensor_scalar(r8[:, 0], r8[:, 1], -1.0, 1.0, ALU.mult, ALU.add))
            link(nc.vector.tensor_tensor(r8[:, 2], lg[:, :, :], r8[:, 0], ALU.mult))
            link(nc.vector.scalar_tensor_tensor(out=r8[:, 2], in0=r8[:, 1], scalar=-3.4e38, in1=r8[:, 2],
                                                op0=ALU.mult, op1=ALU.add))
            top(r8[:, 2], r1[:, 1, :], r1[:, 6, :], r8[:, 0], r8[:, 3])
            nc.vector.tensor_tensor(r1[:, 3, :], r1[:, 1, :], r1[:, 0, :], ALU.subtract).then_inc(gap_done, 1)
            dve.wait_ge(gexp_done, 1)
            link(nc.vector.tensor_scalar(r1[:, 2, :], r1[:, 4, :], 1.0, None, ALU.add))
            link(nc.vector.reciprocal(r1[:, 7, :], r1[:, 2, :]))
            link(nc.vector.tensor_scalar(r1[:, 2, :], r1[:, 7, :], sc[:, 20:21], None, ALU.mult))
            link(nc.vector.tensor_tensor(r1[:, 7, :], r1[:, 2, :], r1[:, 4, :], ALU.mult))
            link(nc.vector.tensor_tensor(r8[:, 1], r8[:, 1], over_e(r1[:, 2, :]), ALU.mult))
            link(nc.vector.tensor_tensor(r8[:, 3], r8[:, 3], over_e(r1[:, 7, :]), ALU.mult))
            link(nc.vector.tensor_tensor(routed[:, :, :], r8[:, 1], r8[:, 3], ALU.add))

            for w, (hi, lo) in enumerate(((w1h[:].rearrange("p e h -> p (e h)"), w1l[:].rearrange("p e h -> p (e h)")),
                                          (w2h[:].rearrange("p e c d -> p (e c d)"), w2l[:].rearrange("p e c d -> p (e c d)")))):
                dve.wait_ge(whi_done, w + 1)
                nc.vector.scalar_tensor_tensor(out=lo, in0=wf[:, w], scalar=sc[:, 12 + w:13 + w], in1=hi,
                                               op0=ALU.mult, op1=ALU.subtract).then_inc(wlo_done, 1)

            def low(b, e):
                for c in range(HC):
                    n = b * (E * HC) + (e * HC + c)
                    dve.wait_ge(hi_done, n + 1)
                    dve.wait_ge(down_done, b * E + (e + 1))
                    nc.vector.tensor_tensor(hl[:, e % 2, c], h32[:, e % 2, c], hh[:, e % 2, c], ALU.subtract).then_inc(lo_done, 1)

            def gate(b, e):
                dve.wait_ge(down_done, b * E + (e + 3))
                for s in range(SUB):
                    t = b * SUB + s
                    dve.wait_ge(acc_done, (b * E + (e + 1)) * SUB + (s + 1))
                    xt = x[:, bass.ds(t, 1), :].rearrange("p a d -> p (a d)")
                    nc.vector.scalar_tensor_tensor(out=xt, in0=ps[:, 4 + e % 2, s * P:(s + 1) * P],
                                                   scalar=routed[:, bass.ds(t, 1), e], in1=xt,
                                                   op0=ALU.mult, op1=ALU.add).then_inc(acc_done, 1)

            with dve.Fori(0, NB) as b:
                for e in range(E):
                    low(b, e)
                    if e >= 1:
                        gate(b, e - 1)
                gate(b, E - 1)

        @block.tensor
        def _(pe):
            pe.wait_ge(const_done, 6)
            pe.wait_ge(small_in[5], 16)
            nc.tensor.transpose(ps[:, 6, 0:E * HC], b1r[:, :], ident[0:E * HC, 0:E * HC]).then_inc(b1T_done, 1)

            def turn(bank, par, done):
                for a in range(TPU):
                    ins = nc.tensor.transpose(ps[:, bank, a * P:(a + 1) * P], xn_s[:, par, a], ident[:, :])
                ins.then_inc(done, 1)

            def turn_x(u, par):
                pe.wait_ge(norm_done, u + 1)
                turn(par, par, xT_done)

            turn_x(0, 0)
            turn_x(1, 1)
            pe.wait_ge(wq_in, 16)

            def qkv(it, last):
                for par in range(2):
                    u = it * 2 + par
                    pe.wait_ge(xT_out, u + 1)
                    pe.wait_ge(qkv_free, u * 2 + 2)
                    for a in range(TPU):
                        ins = nc.tensor.matmul(ps[:, 2 + 2 * par + a, 0:3 * D], xT_s[:, par, a * P:(a + 1) * P], wqkv[:, :],
                                               start=True, stop=True)
                    ins.then_inc(qkv_done, 1)
                if not last:
                    for par in range(2):
                        turn_x(it * 2 + par + 2, par)

            with pe.Fori(0, U // 2 - 1) as it:
                qkv(it, False)
            qkv(U // 2 - 1, True)

            pe.wait_ge(qkv_free, 2 * U + 4)

            def prefix(u, par):
                for a in range(TPU):
                    pe.wait_ge(kv_done, u * TPU + (a + 1))
                    pe.wait_ge(m_done, u * TPU + (a + 1))
                    for g, (h0, h1) in enumerate(HEADS):
                        o = ps[:, 3 * a + g, 0:(h1 - h0) * KV]
                        kv = [kv_s[:, par, b, h0:h1, :].rearrange("p h n -> p (h n)") for b in range(TPU)]
                        if a == 1:
                            nc.tensor.matmul(o, ones[:, :], kv[0], start=True, stop=False)
                        ins = nc.tensor.matmul(o, tri[:, :], kv[a], start=(a == 0), stop=True)
                    ins.then_inc(pfx_done, 1)

            units(pe, prefix, 0, U)

            def turn_y(u, par):
                pe.wait_ge(y_done, u + 1)
                turn(par, par, yT_done)

            turn_y(0, 0)
            turn_y(1, 1)
            pe.wait_ge(small_in[2], 16)

            def proj(it, last):
                for par in range(2):
                    u = it * 2 + par
                    pe.wait_ge(yT_out, u + 1)
                    pe.wait_ge(x2_done, u + 1)
                    for a in range(TPU):
                        ins = nc.tensor.matmul(ps[:, 2 + par, a * P:(a + 1) * P], xT_s[:, par, a * P:(a + 1) * P], wproj[:, :],
                                               start=True, stop=True)
                    ins.then_inc(proj_done, 1)
                if not last:
                    for par in range(2):
                        turn_y(it * 2 + par + 2, par)

            with pe.Fori(0, U // 2 - 1) as it:
                proj(it, False)
            proj(U // 2 - 1, True)

            def turn_x2(u, par):
                pe.wait_ge(norm2_done, u + 1)
                turn(4 + par, par, x2T_done)

            turn_x2(0, 0)
            turn_x2(1, 1)
            pe.wait_ge(small_in[3], 16)

            def router(it, last):
                for par in range(2):
                    u = it * 2 + par
                    pe.wait_ge(x2T_out, u + 1)
                    pe.wait_ge(lgs_done, u + 1)
                    for a in range(TPU):
                        ins = nc.tensor.matmul(ps[:, 6 + par, a * E:(a + 1) * E], xT_s[:, par, a * P:(a + 1) * P], wr[:, :],
                                               start=True, stop=True)
                    ins.then_inc(lg_done, 1)
                if not last:
                    for par in range(2):
                        pe.wait_ge(xh_done, it * 2 + (par + 1))
                        turn_x2(it * 2 + par + 2, par)

            with pe.Fori(0, U // 2 - 1) as it:
                router(it, False)
            router(U // 2 - 1, True)

            pe.wait_ge(xl_done, U + 2)
            pe.wait_ge(wlo_done, 2)
            pe.wait_ge(b2_in, 16 * 3)

            def up(b, e):
                xh, xl = (v[:, bass.ds(b * TOK, TOK)] for v in (xTh, xTl))
                for c in range(HC):
                    n = b * (E * HC) + (e * HC + c)
                    pe.wait_ge(relu1_done, n + 1)
                    cs = slice(c * P, (c + 1) * P)
                    nc.tensor.matmul(ps[:, c, :], w1h[:, e, cs], xh, start=True, stop=False)
                    nc.tensor.matmul(ps[:, c, :], w1h[:, e, cs], xl, start=False, stop=False)
                    nc.tensor.matmul(ps[:, c, :], w1l[:, e, cs], xh, start=False, stop=True).then_inc(up_done, 1)

            def down(b, e):
                pe.wait_ge(acc_done, (b * E + (e + 1)) * SUB)
                pe.wait_ge(lo_done, (b * E + (e + 3)) * HC)
                for s in range(SUB):
                    o = ps[:, 4 + e % 2, s * P:(s + 1) * P]
                    tok = slice(s * P, (s + 1) * P)
                    nc.tensor.matmul(o, ones3[:, :], b2p[:, e, :], start=True, stop=False)
                    for c in range(HC):
                        nc.tensor.matmul(o, hh[:, e % 2, c, tok], w2h[:, e, c, :], start=False, stop=False)
                        nc.tensor.matmul(o, hh[:, e % 2, c, tok], w2l[:, e, c, :], start=False, stop=False)
                        ins = nc.tensor.matmul(o, hl[:, e % 2, c, tok], w2h[:, e, c, :], start=False, stop=(c == HC - 1))
                ins.then_inc(down_done, 1)

            with pe.Fori(0, NB) as b:
                up(b, 0)
                for e in range(E):
                    if e + 1 < E:
                        up(b, e + 1)
                    down(b, e)


_INS = ['L0_attn_x', 'L0_attn_W_attn', 'L0_attn_b_attn', 'L0_attn_W_proj', 'L0_attn_b_proj', 'L0_ffn_W1', 'L0_ffn_b1',
        'L0_ffn_W2', 'L0_ffn_b2', 'L0_ffn_Wr', 'L0_ffn_br']


def kernel(**inputs):
    import numpy as _np
    import concourse.bacc as _bacc
    from concourse import mybir as _mybir
    from concourse.bass_utils import run_bass_kernel_spmd as _run

    nc = _bacc.Bacc("TRN2", target_bir_lowering=False, num_devices=1)
    arrays, args = {}, []
    for name in _INS:
        a = _np.ascontiguousarray(inputs[name])
        arrays[f"in_{name}_dram"] = a
        args.append(nc.dram_tensor(f"in_{name}_dram", a.shape, _mybir.dt.from_np(a.dtype), kind="ExternalInput").ap())
    out = nc.dram_tensor("out_dram", inputs['L0_attn_x'].shape, F32, kind="ExternalOutput").ap()
    block_kernel(nc, *args, out)
    r = _run(nc, [arrays], core_ids=[0])
    return r.results[0]["out_dram"]
```

```python
from contextlib import ExitStack

import concourse.bass as bass
from concourse import mybir

F32 = mybir.dt.float32
F16 = mybir.dt.float16
BF16 = mybir.dt.bfloat16
I32 = mybir.dt.int32
ALU = mybir.AluOpType
ACT = mybir.ActivationFunctionType
AX = mybir.AxisListType


def block_kernel(nc, x_d, wqkv_d, bqkv_d, wproj_d, bproj_d, w1_d, b1_d, w2_d, b2_d, wr_d, br_d, out_d):
    P = 128
    SEQS, T, D = x_d.shape
    NT = SEQS * T // P
    U = SEQS
    TPU = T // P
    H, DH = 16, D // 16
    E, _, HID = w1_d.shape
    HC = HID // P
    DV = DH + 1
    KV = DV * DH
    LN_EPS, DEN_EPS = 1e-5, 1e-6
    LOADS = 4
    TPL = NT // LOADS
    assert TPU == 2 and D == P and U % 2 == 0

    HEADS = [(0, 6), (6, 11), (11, 16)]
    X_SCALE = 2.0 ** 4
    W_TOP = 2.0 ** 9
    H_TOP = 2.0 ** 14
    TOP = 2
    GPB = 2
    SLOTS = GPB * P
    RT = [16, NT - 16]
    R = len(RT)
    T0 = [sum(RT[:r]) for r in range(R)]
    RB = [TOP * n // GPB + E - 1 for n in RT]
    B0 = [sum(RB[:r]) for r in range(R)]
    NBLK = sum(RB)
    EXPERT_BLOCKS = -(-max(RT) * P // SLOTS)
    BODY = 2
    ITERS = NBLK // BODY
    MIX = 2
    PAIRS = RT[0] // (2 * MIX) - 1
    MIX_FROM = ITERS - 2 * PAIRS
    TAIL = 8
    MID = NT * P // 2
    assert NBLK % BODY == 0 and RT[0] == (PAIRS + 1) * 2 * MIX and MIX_FROM * BODY >= RB[0] + 2 and RT[1] % TAIL == 0 and TAIL == 4 * MIX

    xv = x_d.rearrange("s (a p) d -> p (s a) d", p=P)
    ov = out_d.rearrange("s (a p) d -> p (s a) d", p=P)

    x2_rows = nc.dram_tensor("x2_rows", [NT * P, D], F32).ap()
    y_rows = nc.dram_tensor("y_rows", [NBLK * SLOTS, D], F32).ap()
    b2_parts = nc.dram_tensor("b2_parts", [3, E, D], BF16).ap()
    yv = y_rows.rearrange("(b g p) d -> p b g d", g=GPB, p=P)
    x2v = x2_rows.rearrange("(t p) c -> p t c", p=P)

    with ExitStack() as ctx:
        def sb(name, shape, dt=F32):
            return ctx.enter_context(nc.sbuf_tensor(name, shape, dt))

        def sem(name):
            return ctx.enter_context(nc.semaphore(name))

        ps = ctx.enter_context(nc.psum_tensor("ps", [P, 8, 512], F32))

        x = sb("x", [P, NT, D])
        wqkv = sb("wqkv", [P, 3 * D])
        bqkv = sb("bqkv", [P, 3 * D])
        wproj = sb("wproj", [P, D])
        bproj = sb("bproj", [P, D])
        wr = sb("wr", [P, E])
        br = sb("br", [P, E])
        w1h = sb("w1h", [P, E, HID], F16)
        w1l = sb("w1l", [P, E, HID], F16)
        w2 = sb("w2", [P, E, HC, 2, D], F16)
        wf = sb("wf", [P, 2, E * HID])
        b1r = sb("b1r", [E * HC, P])
        b1T = sb("b1T", [P, E * HC])
        b1s = sb("b1s", [P, E * HC])
        b2p = sb("b2p", [3, E, D], BF16)
        ones3 = sb("ones3", [3, P], BF16)
        ident = sb("ident", [P, P])
        tri = sb("tri", [P, P])
        ones = sb("ones", [P, P])
        neghalf = sb("neghalf", [P, NT])
        iota_i = sb("iota_i", [P, E], I32)
        iota = sb("iota", [P, E])
        st = sb("st", [P, NT, 6])
        lnt = sb("lnt", [P, 7, NT])
        rstd = sb("rstd", [P, 2, NT])
        xn_s = sb("xn_s", [P, 2, TPU, D])
        xT_s = sb("xT_s", [P, 2, T])
        work = sb("work", [P, 2 * H * KV])
        qk = sb("qk", [P, NT, 2 * D])
        vaug = sb("vaug", [P, NT, H, DV])
        kv_s = sb("kv_s", [P, 2, TPU, H, KV])
        nd = sb("nd", [P, NT, H * DV])
        rd = sb("rd", [P, NT, H])
        lg = sb("lg", [P, NT, E])
        r8 = sb("r8", [P, 4, NT, E])
        r1 = sb("r1", [P, 8, NT])
        ident_h = sb("ident_h", [P, P], F16)
        ones_h = sb("ones_h", [P, P], F16)
        before_h = sb("before_h", [P, P], F16)
        count_i = sb("count_i", [P, P], I32)
        slot_of = sb("slot_of", [P, P], F16)
        group_of = sb("group_of", [P, NBLK * GPB], F16)
        block_f = sb("block_f", [P, NBLK])
        full_at = sb("full_at", [P, EXPERT_BLOCKS])
        token_of = sb("token_of", [P, NT], F16)
        in_round = sb("in_round", [P, E, NT])
        in_row = sb("in_row", [P, R, E])
        b2hml = sb("b2hml", [E, 3, D], BF16)
        sc = sb("sc", [P, 24])
        ndf = nd[:, :, :].rearrange("p t n -> p (t n)")
        kvf = kv_s[:, :, :, :, :].rearrange("p b a h n -> p (b a h n)")
        w2f = w2[:, :, :, :, :].rearrange("p e c w d -> p (e c w d)")
        w2p = w2[:, :, :, :, :].rearrange("p e c w d -> p (e c) w d")
        wf2 = wf[:, 1].rearrange("p (n d) -> p n d", d=D)
        b2r, b2s, b2f = (kvf[0:E, n * D:(n + 1) * D] for n in range(3))
        te = work[:, 0:4 * T * 2].rearrange("p (w a t d) -> p w a t d", w=2, a=2, t=TPU)
        t_s, e_s = te[:, 0], te[:, 1]
        m_s = work[:, :].rearrange("p (a n) -> p a n", a=2)

        def places(region):
            at = [0]

            def place(n, dt=F32):
                words = n if dt in (F32, I32) else n // 2
                at[0] += words
                assert at[0] <= region.shape[1]
                v = region[:, at[0] - words:at[0]]
                return v if dt == F32 else v.bitcast(dt)
            return place

        in_qk = places(qk[:, :, :].rearrange("p t d -> p (t d)"))
        x2_words = in_qk(2 * TPU * D)
        x2row = x2_words.bitcast(F16).rearrange("p (b a c) -> p b a c", b=2, a=TPU)
        slot_hot = in_qk(TOP * NT * P, F16).rearrange("p (c t s) -> p c t s", c=TOP, t=NT)
        HG = RB[0] * GPB
        group_hot = in_qk(TOP * NT * HG, F16).rearrange("p (c t n) -> p c t n", c=TOP, t=NT)
        group_eq = in_qk(TOP * NT * HG, F16).rearrange("p (c t n) -> p c t n", c=TOP, t=NT)
        in_nd = places(ndf)
        pre = in_nd(2 * HC * SLOTS).rearrange("p (b c n) -> p b c n", b=2, c=HC)
        hh = in_nd(2 * HC * SLOTS, F16).rearrange("p (b c n) -> p b c n", b=2, c=HC)
        hl = in_nd(2 * HC * SLOTS, F16).rearrange("p (b c n) -> p b c n", b=2, c=HC)
        in_work = places(work[:, :])
        xg_words = in_work(2 * GPB * D)
        xg = xg_words.bitcast(F16).rearrange("p (b g w d) -> p b g w d", b=2, g=GPB, w=2)
        xgT = in_work(2 * 2 * SLOTS, F16).rearrange("p (b w n) -> p b w n", b=2, w=2)
        y_low = in_work(2 * GPB * D).rearrange("p (b g d) -> p b g d", b=2, g=GPB)
        in_v = places(vaug[:, :, :, :].rearrange("p t h d -> p (t h d)"))
        ysb = in_v(2 * GPB * D).rearrange("p (b g d) -> p b g d", b=2, g=GPB)
        yg = in_v(TAIL * TOP * D).rearrange("p (b c d) -> p b c d", b=TAIL, c=TOP)
        ids = in_v(NBLK * GPB, I32)
        ix = in_v(2 * GPB, I32).rearrange("p (b g) -> p b g", b=2)
        ixy = in_v(TAIL * TOP, I32).rearrange("p (b c) -> p b c", b=TAIL)
        expert_i = in_v(ITERS * (BODY + 2), I32).rearrange("p (i j) -> p i j", j=BODY + 2)
        pos_i = in_v(NT * TOP, I32).rearrange("p (t c) -> p t c", c=TOP)
        part_i = in_v(2 * NT * TOP, I32).rearrange("p (w t c) -> p w t c", w=2, c=TOP)
        part_h = in_v(2 * NT * TOP, F16).rearrange("p (w t c) -> p w t c", w=2, c=TOP)
        pos_f = in_v(NT * TOP).rearrange("p (t c) -> p t c", c=TOP)
        picked = in_v(NT * E, F16).rearrange("p (t e) -> p t e", e=E)
        tot, upto, ahead = (in_v(E * NT).rearrange("p (e t) -> p e t", e=E) for _ in range(3))
        pos8 = in_v(NT * E).rearrange("p (t e) -> p t e", e=E)
        cnt, nblk, ends, base = (in_v(R * E).rearrange("p (r e) -> p r e", r=R) for _ in range(4))
        full = in_v(R * E * EXPERT_BLOCKS).rearrange("p (r e j) -> p r e j", r=R, e=E)
        slot_past = in_qk(RB[0] * E)
        expert_f = in_qk(NBLK)

        x_in = [sem(f"x_in{g}") for g in range(LOADS)]
        wq_in = sem("wq_in")
        w1_in = sem("w1_in")
        w2_in = sem("w2_in")
        small_in = [sem(f"small_in{g}") for g in range(7)]
        const_done = sem("const_done")
        table_done = sem("table_done")
        chain = sem("chain")
        pchain = sem("pchain")
        achain = sem("achain")
        stats_done = sem("stats_done")
        rstd_done = sem("rstd_done")
        bn_done = sem("bn_done")
        norm_done = sem("norm_done")
        xT_done = sem("xT_done")
        xT_out = sem("xT_out")
        qkv_done = sem("qkv_done")
        qkv_free = sem("qkv_free")
        t_done = sem("t_done")
        relu_done = sem("relu_done")
        exp_done = sem("exp_done")
        phi_done = sem("phi_done")
        kv_done = sem("kv_done")
        pfx_done = sem("pfx_done")
        m_done = sem("m_done")
        red_done = sem("red_done")
        xb_done = sem("xb_done")
        y_done = sem("y_done")
        yT_done = sem("yT_done")
        yT_out = sem("yT_out")
        proj_done = sem("proj_done")
        x2_done = sem("x2_done")
        var2_done = sem("var2_done")
        norm2_done = sem("norm2_done")
        x2T_done = sem("x2T_done")
        x2T_out = sem("x2T_out")
        lg_done = sem("lg_done")
        lgs_done = sem("lgs_done")
        gap_done = sem("gap_done")
        gexp_done = sem("gexp_done")
        b1T_done = sem("b1T_done")
        b1T_out = sem("b1T_out")
        wabs_done = sem("wabs_done")
        wmax_done = sem("wmax_done")
        wall_done = sem("wall_done")
        scale_done = sem("scale_done")
        whi_done = sem("whi_done")
        wscaled_done = sem("wscaled_done")
        wlo_done = sem("wlo_done")
        b2_done = sem("b2_done")
        b2_in = sem("b2_in")
        out_done = sem("out_done")
        xh_done = sem("xh_done")
        xl_done = sem("xl_done")
        x2_stored = [sem(f"x2_stored{b}") for b in range(2)]
        picked_done = sem("picked_done")
        count_done = sem("count_done")
        part_done = sem("part_done")
        slot_hot_done = sem("slot_hot_done")
        group_eq_done = sem("group_eq_done")
        group_hot_done = sem("group_hot_done")
        inverse_done = sem("inverse_done")
        ids_done = sem("ids_done")
        expert_done = sem("expert_done")
        ix_done = sem("ix_done")
        ixy_done = sem("ixy_done")
        gathered = [sem(f"gathered{b}") for b in range(2)]
        turn_done = sem("turn_done")
        turn_out = sem("turn_out")
        up_done = sem("up_done")
        pre_done = sem("pre_done")
        hi_done = sem("hi_done")
        lo_done = sem("lo_done")
        down_done = sem("down_done")
        y_low_done = sem("y_low_done")
        y_done2 = sem("y_done2")
        y_stored = [sem(f"y_stored{b}") for b in range(2)]
        y_gathered = [sem(f"y_gathered{b}") for b in range(TAIL)]
        mix_half = sem("mix_half")
        mix_done = sem("mix_done")

        block = ctx.enter_context(nc.Block())

        def stored_before(n, b):
            return len(range(b, n, 2))

        def units(eng, body, first, end):
            with eng.Fori(first // 2, end // 2) as it:
                for par in range(2):
                    body(it * 2 + par, par)

        def exists(n):
            return not isinstance(n, int) or n < NBLK

        def expert_registers(eng, which):
            return [eng.alloc_register(name=f"{which}_expert{j}") for j in range(BODY + 2)]

        def load_experts(eng, regs, it):
            eng.load(regs, expert_i[0:1, bass.ds(it, 1), :].rearrange("p a j -> p (a j)"))

        def expert(eng, regs, j):
            return eng.snap(regs[j], min_val=0, max_val=E - 1)

        def tiles(t, u):
            return t[:, bass.ds(u * TPU, TPU)]

        @block.sync
        def _(sp):
            for g in range(LOADS):
                sp.dma_start(x[:, g * TPL:(g + 1) * TPL, :], xv[:, g * TPL:(g + 1) * TPL, :]).then_inc(x_in[g], 16)
            sp.dma_start(wf[:, 0, :].rearrange("p (e h) -> p e h", e=E), w1_d.rearrange("e d h -> d e h")).then_inc(w1_in, 16)
            sp.dma_start(wf[:, 1, :].rearrange("p (e c d) -> p e c d", e=E, c=HC),
                         w2_d.rearrange("e (c p) d -> p e c d", p=P)).then_inc(w2_in, 16)
            sp.wait_ge(pfx_done, NT + 2 * TPU)
            sp.dma_start(b2r, b2_d).then_inc(small_in[6], 16)
            sp.wait_ge(b2_done, 1)
            sp.dma_start(b2_parts.rearrange("r e d -> e r d"), b2hml[:, :, :]).then_inc(b2_in, 16)
            sp.wait_ge(b2_in, 16)
            sp.dma_start(b2p[:, :, :], b2_parts).then_inc(b2_in, 16)

            def store_x2(u, par):
                sp.wait_ge(xl_done, u + 1)
                sp.dma_start(x2v[:, bass.ds(u * TPU, TPU), :], x2_words.rearrange("p (b a d) -> p b a d", b=2, a=TPU)[:, par]).then_inc(x2_stored[par], 16)

            units(sp, store_x2, 0, U)

            def store_y(n, j):
                sp.wait_ge(y_done2, n + 3)
                sp.dma_start(yv[:, bass.ds(n, 1)].rearrange("p a g d -> p (a g) d"), ysb[:, j]).then_inc(y_stored[j], 16)

            def store_out(t, n):
                sp.wait_ge(mix_done, t + (n + TAIL))
                sp.dma_start(ov[:, bass.ds(t, n), :], x[:, bass.ds(t, n), :]).then_inc(out_done, 16)

            with sp.Fori(0, MIX_FROM) as it:
                for j in range(BODY):
                    store_y(it * BODY + j, j)
            with sp.Fori(0, PAIRS) as q:
                for half in range(2):
                    for j in range(BODY):
                        store_y(q * (2 * BODY) + ((MIX_FROM + half) * BODY + j), j)
                    store_out(q * (2 * MIX) + half * MIX, MIX)
            store_out(PAIRS * 2 * MIX, 2 * MIX)
            with sp.Fori(0, RT[1] // TAIL) as it:
                for s in range(TAIL):
                    store_out(it * TAIL + (T0[1] + s), 1)
            sp.wait_ge(out_done, 16 * (2 * PAIRS + 1 + RT[1]))

        @block.gpsimd
        def _(pool):
            nc.gpsimd.memset(ident[:], 0.0).then_inc(pchain, 1)
            nc.gpsimd.memset(ones[:], 1.0).then_inc(pchain, 1)
            nc.gpsimd.memset(ones3[:], 1.0).then_inc(const_done, 1)
            nc.gpsimd.memset(neghalf[:], -0.5).then_inc(const_done, 1)
            nc.gpsimd.memset(vaug[:, :, :, DH:DV], 1.0).then_inc(const_done, 1)
            nc.gpsimd.iota(iota_i[:], [[1, E]], base=0, channel_multiplier=0).then_inc(pchain, 1)
            pool.wait_ge(pchain, 3)
            nc.gpsimd.affine_select(out=ident[:], in_=ident[:], compare_op=ALU.not_equal, fill=1.0, base=0,
                                    pattern=[[-1, P]], channel_multiplier=1).then_inc(const_done, 1)
            nc.gpsimd.affine_select(out=tri[:], in_=ones[:], compare_op=ALU.is_ge, fill=0.0, base=0,
                                    pattern=[[1, P]], channel_multiplier=-1).then_inc(const_done, 1)
            nc.gpsimd.tensor_copy(iota[:], iota_i[:]).then_inc(const_done, 1)

            nc.gpsimd.memset(ones_h[:], 1.0).then_inc(table_done, 1)
            nc.gpsimd.memset(in_round[:], 1.0).then_inc(table_done, 1)
            nc.gpsimd.memset(in_row[:], 1.0).then_inc(table_done, 1)
            nc.gpsimd.iota(count_i[:], [[1, P]], base=0, channel_multiplier=0).then_inc(table_done, 1)
            pool.wait_ge(const_done, 6)
            pool.wait_ge(table_done, 4)
            nc.gpsimd.tensor_copy(ident_h[:], ident[:]).then_inc(table_done, 1)
            nc.gpsimd.affine_select(out=before_h[:], in_=ones_h[:], compare_op=ALU.is_ge, fill=0.0, base=-1,
                                    pattern=[[1, P]], channel_multiplier=-1).then_inc(table_done, 1)
            for r in range(R):
                nc.gpsimd.memset(in_round[:, :, T0[r]:T0[r] + 1], 0.0).then_inc(table_done, 1)
            nc.gpsimd.memset(in_row[:, :, 0:1], 0.0).then_inc(table_done, 1)
            nc.gpsimd.tensor_copy(slot_of[:], count_i[:]).then_inc(table_done, 1)
            nc.gpsimd.tensor_copy(group_of[:], count_i[:, 0:NBLK * GPB]).then_inc(table_done, 1)
            nc.gpsimd.tensor_copy(block_f[:], count_i[:, 0:NBLK]).then_inc(table_done, 1)
            nc.gpsimd.tensor_scalar(full_at[:], count_i[:, 0:EXPERT_BLOCKS], float(SLOTS), None, ALU.mult).then_inc(table_done, 1)
            pool.wait_ge(table_done, 13)
            nc.gpsimd.iota(count_i[:, 0:NT], [[P, NT]], base=-MID, channel_multiplier=1).then_inc(table_done, 1)
            pool.wait_ge(table_done, 14)
            nc.gpsimd.tensor_copy(token_of[:], count_i[:, 0:NT]).then_inc(table_done, 1)

            pool.wait_ge(const_done, 6)
            for g in range(LOADS):
                gt = slice(g * TPL, (g + 1) * TPL)
                pool.wait_ge(stats_done, g + 1)
                nc.gpsimd.tensor_tensor(rstd[:, 0, gt], lnt[:, 4, gt], neghalf[:, gt], ALU.pow).then_inc(rstd_done, 1)

            def kv_products(u, par):
                pool.wait_ge(phi_done, u + 3)
                pool.wait_ge(pfx_done, u * 2 + 2)
                for a in range(TPU):
                    k = qk[:, bass.ds(u * TPU + a, 1), D:2 * D].rearrange("p a (h i) -> p (a h) i", i=DH)
                    v = vaug[:, bass.ds(u * TPU + a, 1), :, :].rearrange("p a h j -> p (a h) j")
                    nc.gpsimd.tensor_tensor(kv_s[:, par, a].rearrange("p h (j i) -> p h j i", j=DV),
                                            k.unsqueeze(2).broadcast_to([P, H, DV, DH]),
                                            v.unsqueeze(3).broadcast_to([P, H, DV, DH]), ALU.mult).then_inc(kv_done, 1)

            units(pool, kv_products, 0, U // 4)
            pool.wait_ge(wmax_done, 3)
            nc.gpsimd.partition_all_reduce(sc[:, 4:7], sc[:, 0:3], P, bass.bass_isa.ReduceOp.max).then_inc(wall_done, 1)
            units(pool, kv_products, U // 4, U)
            pool.wait_ge(small_in[1], 16)
            for g in range(LOADS):
                xg = x[:, g * TPL:(g + 1) * TPL, :]
                nc.gpsimd.tensor_tensor(xg, xg, bproj[:, :].unsqueeze(1).broadcast_to([P, TPL, D]), ALU.add).then_inc(xb_done, 1)

            for half in range(2):
                ht = slice(half * NT // 2, (half + 1) * NT // 2)
                pool.wait_ge(var2_done, half + 1)
                nc.gpsimd.tensor_tensor(rstd[:, 1, ht], lnt[:, 4, ht], neghalf[:, ht], ALU.pow).then_inc(rstd_done, 1)

            pool.wait_ge(wscaled_done, 1)
            nc.gpsimd.tensor_tensor(w1l[:].rearrange("p e h -> p (e h)"), wf[:, 0], w1h[:].rearrange("p e h -> p (e h)"),
                                    ALU.subtract).then_inc(wlo_done, 1)
            pool.wait_ge(wscaled_done, 2)
            nc.gpsimd.tensor_tensor(w2p[:, :, 1], wf2, w2p[:, :, 0], ALU.subtract).then_inc(wlo_done, 1)

            for r in range(R):
                rt = slice(T0[r], T0[r] + RT[r])
                for c in range(TOP):
                    pool.wait_ge(group_eq_done, r * TOP + (c + 1))
                    nc.gpsimd.tensor_tensor(group_hot[:, c, rt, 0:RB[r] * GPB], group_eq[:, c, rt, 0:RB[r] * GPB],
                                            token_of[:, rt].unsqueeze(2).broadcast_to([P, RT[r], RB[r] * GPB]),
                                            ALU.mult).then_inc(group_hot_done, 1)

            for b in range(2):
                pool.wait_ge(x2_stored[b], 16 * (U // 2 + 1))

            def gather_x(n, j):
                pool.wait_ge(turn_done, n + 1)
                nc.gpsimd.tensor_copy(ix[:, j], ids[:, bass.ds(n * GPB, GPB)]).then_inc(ix_done, 1)
                pool.wait_ge(ix_done, n + 1)
                pool.nop(nofuse=True)
                for g in range(GPB):
                    at = (j * GPB + g) * D
                    nc.gpsimd.indirect_dma_start(out=xg_words[:, at:at + D], out_offset=None, in_=x2_rows,
                                                 in_offset=bass.IndirectOffsetOnAxis(ap=ix[:, j, g:g + 1], axis=0)
                                                 ).then_inc(gathered[j], 16)

            def gather_y(call, t, n, first, slots, rows):
                pool.wait_ge(mix_done, t + (n + TAIL - slots))
                nc.gpsimd.tensor_copy(ixy[:, first:first + n, :], pos_i[:, bass.ds(t, n), :]).then_inc(ixy_done, 1)
                pool.wait_ge(ixy_done, call + 1)
                pool.nop(nofuse=True)
                for s in range(first, first + n):
                    for c in range(TOP):
                        nc.gpsimd.indirect_dma_start(out=yg[:, s, c], out_offset=None, in_=rows,
                                                     in_offset=bass.IndirectOffsetOnAxis(ap=ixy[:, s, c:c + 1], axis=0)
                                                     ).then_inc(y_gathered[s], 16)

            def gather_first(q, half):
                for b in range(2):
                    pool.wait_ge(y_stored[b], 16 * (1 + stored_before(RB[0], b)))
                gather_y(q * 2 + half, q * (2 * MIX) + half * MIX, MIX, half * MIX, 2 * MIX, y_rows[0:RB[0] * SLOTS, :])

            pool.wait_ge(ids_done, 1)
            with pool.Fori(0, MIX_FROM) as it:
                for j in range(BODY):
                    gather_x(it * BODY + j, j)

            pool.wait_ge(ids_done, 2)
            with pool.Fori(0, PAIRS) as q:
                for half in range(2):
                    for j in range(BODY):
                        gather_x(q * (2 * BODY) + ((MIX_FROM + half) * BODY + j), j)
                    gather_first(q, half)
            for half in range(2):
                gather_first(PAIRS, half)
            for b in range(2):
                pool.wait_ge(y_stored[b], 16 * (1 + stored_before(NBLK, b)))
            with pool.Fori(0, RT[1] // TAIL) as it:
                for half in range(2):
                    gather_y(it * 2 + (2 * PAIRS + 2 + half), it * TAIL + (T0[1] + half * 2 * MIX), 2 * MIX,
                             (1 - half) * 2 * MIX, TAIL, y_rows)

        @block.scalar
        def _(act):
            act.dma_start(wqkv[:, :], wqkv_d).then_inc(wq_in, 16)
            act.dma_start(bqkv[:, :], bqkv_d.partition_broadcast(P)).then_inc(small_in[0], 16)
            act.dma_start(bproj[:, :], bproj_d.partition_broadcast(P)).then_inc(small_in[1], 16)
            act.dma_start(wproj[:, :], wproj_d).then_inc(small_in[2], 16)
            act.dma_start(wr[:, :], wr_d).then_inc(small_in[3], 16)
            act.dma_start(br[:, :], br_d.partition_broadcast(P)).then_inc(small_in[4], 16)
            act.dma_start(b1r[:, :], b1_d.rearrange("e (c p) -> (e c) p", p=P)).then_inc(small_in[5], 16)

            def copy_xT(u, par):
                act.wait_ge(xT_done, u + 1)
                nc.scalar.activation(xT_s[:, par, :], ps[:, par, 0:T], ACT.Copy).then_inc(xT_out, 1)

            copy_xT(0, 0)
            copy_xT(1, 1)

            def features(it, last):
                for par in range(2):
                    u = it * 2 + par
                    act.wait_ge(t_done, u + 1)
                    nc.scalar.activation(e_s[:, par], t_s[:, par], ACT.Relu, scale=-1.0).then_inc(relu_done, 1)
                    act.wait_ge(relu_done, u + 1)
                    nc.scalar.activation(e_s[:, par], e_s[:, par], ACT.Exp, scale=-1.0).then_inc(exp_done, 1)
                    if not last:
                        act.wait_ge(qkv_done, u + 1)
                        copy_xT(u + 2, par)

            with act.Fori(0, U // 2 - 1) as it:
                features(it, False)
            features(U // 2 - 1, True)

            act.wait_ge(b1T_done, 1)
            nc.scalar.activation(b1T[:, :], ps[:, 6, 0:E * HC], ACT.Copy).then_inc(b1T_out, 1)
            act.wait_ge(b1T_out, 1)

            act.wait_ge(w1_in, 16)
            nc.scalar.activation(w1h[:].rearrange("p e h -> p (e h)").bitcast(BF16), wf[:, 0], ACT.Abs).then_inc(wabs_done, 1)
            act.wait_ge(w2_in, 16)
            nc.scalar.activation(w2f[:, 0:E * HID].bitcast(BF16), wf[:, 1], ACT.Abs).then_inc(wabs_done, 1)
            nc.scalar.activation(b1s[:], b1T[:], ACT.Abs).then_inc(wabs_done, 1)

            act.wait_ge(scale_done, 1)
            nc.scalar.activation(w1h[:].rearrange("p e h -> p (e h)"), wf[:, 0], ACT.Copy, scale=sc[:, 12:13]).then_inc(whi_done, 1)
            nc.scalar.activation(w2p[:, :, 0], wf2, ACT.Copy, scale=sc[:, 13:14]).then_inc(whi_done, 1)
            nc.scalar.activation(b1s[:], b1T[:], ACT.Copy, scale=sc[:, 17:18]).then_inc(achain, 1)
            for w in range(2):
                act.wait_ge(whi_done, w + 1)
                nc.scalar.activation(wf[:, w], wf[:, w], ACT.Copy, scale=sc[:, 12 + w:13 + w]).then_inc(wscaled_done, 1)

            def copy_yT(u, par):
                act.wait_ge(yT_done, u + 1)
                act.wait_ge(proj_done, u + 1)
                nc.scalar.activation(xT_s[:, par, :], ps[:, par, 0:T], ACT.Copy).then_inc(yT_out, 1)

            units(act, copy_yT, 0, U)

            with act.Fori(0, U // 2) as it:
                for par in range(2):
                    u = it * 2 + par
                    act.wait_ge(norm2_done, u + 1)
                    act.wait_ge(x2_stored[par], it * 16 + 16)
                    nc.scalar.activation(x2row[:, par, :, 0:D], xn_s[:, par], ACT.Copy, scale=X_SCALE).then_inc(xh_done, 1)
                for par in range(2):
                    u = it * 2 + par
                    act.wait_ge(x2T_done, u + 1)
                    act.wait_ge(lg_done, u + 1)
                    nc.scalar.activation(xT_s[:, par, :], ps[:, 4 + par, 0:T], ACT.Copy).then_inc(x2T_out, 1)

            act.wait_ge(gap_done, 1)
            nc.scalar.activation(r1[:, 4, :], r1[:, 3, :], ACT.Exp).then_inc(gexp_done, 1)

            act.wait_ge(achain, 1)

            def copy_turned(n, j):
                act.wait_ge(turn_done, n + 3)
                act.wait_ge(up_done, n + 1)
                nc.scalar.activation(xgT[:, j % 2].rearrange("p w n -> p (w n)"), ps[:, j % 2, :], ACT.Copy).then_inc(turn_out, 1)

            def hidden_high(n, j):
                act.wait_ge(pre_done, n + 3)
                act.wait_ge(down_done, n + 1)
                nc.scalar.activation(hh[:, j % 2], pre[:, j % 2], ACT.Relu).then_inc(hi_done, 1)

            def copy_y_low(n, j):
                act.wait_ge(down_done, n + 3)
                act.wait_ge(y_done2, n + 1)
                nc.scalar.activation(y_low[:, j], ps[:, 6 + j, :].rearrange("p (g w d) -> p g w d", g=GPB, w=2)[:, :, 1],
                                     ACT.Copy).then_inc(y_low_done, 1)

            copy_turned(0, 0)
            copy_turned(1, 1)
            hidden_high(0, 0)
            copy_turned(2, 2)
            copy_turned(3, 3)

            def act_steps(it):
                for j in range(BODY):
                    n = it * BODY + j
                    if exists(n + 1):
                        hidden_high(n + 1, j + 1)
                    copy_y_low(n, j)
                    if exists(n + 4):
                        copy_turned(n + 4, j + 4)

            with act.Fori(0, ITERS - 2) as it:
                act_steps(it)
            act_steps(ITERS - 2)
            act_steps(ITERS - 1)

        @block.vector
        def _(dve):
            count = {"chain": 0}

            def link(ins):
                count["chain"] += 1
                ins.then_inc(chain, 1)
                dve.wait_ge(chain, count["chain"])

            for s, n in ((qkv_free, 4), (phi_done, 2), (pfx_done, 2 * TPU), (m_done, 2), (red_done, 2), (proj_done, 2), (lg_done, 2),
                         (x2_done, 2), (lgs_done, 2), (x2_stored[0], 16), (x2_stored[1], 16), (turn_done, 2), (turn_out, 2),
                         (up_done, 2), (pre_done, 2), (lo_done, 2), (down_done, 2), (y_done2, 2), (mix_done, TAIL),
                         *((s, 16) for s in y_stored)):
                dve.sem_inc(s, n)

            def moments(t0, t1):
                me, qe, mo, qo = (st[:, t0:t1, c] for c in (1, 2, 4, 5))
                l = [lnt[:, c, t0:t1] for c in range(7)]
                nc.vector.tensor_tensor(l[0], me, mo, ALU.add)
                link(nc.vector.tensor_tensor(l[1], me, mo, ALU.subtract))
                nc.vector.tensor_tensor(l[2], qe, qo, ALU.add)
                link(nc.vector.scalar_tensor_tensor(out=l[5], in0=l[1], scalar=0.25, in1=l[1], op0=ALU.mult, op1=ALU.mult))
                nc.vector.tensor_scalar(l[3], l[0], 0.5, None, ALU.mult)
                link(nc.vector.scalar_tensor_tensor(out=l[6], in0=l[2], scalar=1.0 / D, in1=l[5], op0=ALU.mult, op1=ALU.add))
                return nc.vector.tensor_scalar(l[4], l[6], LN_EPS, None, ALU.add)

            def norm(u, par, which, done):
                for a in range(TPU):
                    t = u * TPU + a
                    ins = nc.vector.tensor_scalar(xn_s[:, par, a], x[:, bass.ds(t, 1), :].rearrange("p a d -> p (a d)"),
                                                  lnt[:, 3, bass.ds(t, 1)], rstd[:, which, bass.ds(t, 1)],
                                                  ALU.subtract, ALU.mult)
                ins.then_inc(done, 1)

            for g in range(LOADS):
                dve.wait_ge(x_in[g], 16)
                with dve.Fori(0, TPL // 4) as i:
                    for j in range(4):
                        t = i * 4 + (j + g * TPL)
                        nc.vector.bn_stats(st[:, bass.ds(t, 1), :].rearrange("p a s -> p (a s)"),
                                           x[:, bass.ds(t, 1), :].rearrange("p a d -> p (a d)")).then_inc(bn_done, 1)
                dve.wait_ge(bn_done, (g + 1) * TPL)
                moments(g * TPL, (g + 1) * TPL).then_inc(stats_done, 1)
                dve.wait_ge(stats_done, g + 1)
                if g == 1:
                    dve.wait_ge(rstd_done, 1)
                    norm(0, 0, 0, norm_done)
                    norm(1, 1, 0, norm_done)
            dve.wait_ge(rstd_done, LOADS)
            dve.wait_ge(small_in[0], 16)
            dve.wait_ge(const_done, 6)

            def project_in(it, last):
                for par in range(2):
                    u = it * 2 + par
                    pq = ps[:, 2 + 2 * par:4 + 2 * par, :]
                    dve.wait_ge(qkv_done, u + 1)
                    dve.wait_ge(phi_done, u + 1)
                    nc.vector.tensor_tensor(t_s[:, par], pq[:, :, 0:2 * D],
                                            bqkv[:, 0:2 * D].unsqueeze(1).broadcast_to([P, TPU, 2 * D]),
                                            ALU.add).then_inc(t_done, 1)
                    nc.vector.tensor_tensor(tiles(vaug, u)[:, :, :, 0:DH],
                                            pq[:, :, 2 * D:3 * D].rearrange("p a (h j) -> p a h j", j=DH),
                                            bqkv[:, 2 * D:3 * D].rearrange("p (h j) -> p h j", j=DH).unsqueeze(1)
                                            .broadcast_to([P, TPU, H, DH]), ALU.add).then_inc(qkv_free, 2)
                    if not last:
                        dve.wait_ge(xT_done, u + 1)
                        norm(u + 2, par, 0, norm_done)
                for par in range(2):
                    u = it * 2 + par
                    dve.wait_ge(exp_done, u + 1)
                    nc.vector.scalar_tensor_tensor(out=tiles(qk, u), in0=t_s[:, par], scalar=0.0, in1=e_s[:, par],
                                                   op0=ALU.max, op1=ALU.add).then_inc(phi_done, 1)

            with dve.Fori(0, U // 2 - 1) as it:
                project_in(it, False)
            project_in(U // 2 - 1, True)

            for n, w in enumerate((w1h[:].rearrange("p e h -> p (e h)").bitcast(BF16),
                                   w2f[:, 0:E * HID].bitcast(BF16), b1s[:])):
                dve.wait_ge(wabs_done, n + 1)
                nc.vector.tensor_reduce(sc[:, n:n + 1], w, AX.X, ALU.max).then_inc(wmax_done, 1)

            def attend(u, par):
                for a in range(TPU):
                    t = u * TPU + a
                    dve.wait_ge(pfx_done, t + (2 * TPU + 1))
                    dve.wait_ge(red_done, t + 1)
                    q = qk[:, bass.ds(t, 1), 0:D].rearrange("p a (h i) -> p (a h) i", i=DH)
                    for g, (h0, h1) in enumerate(HEADS):
                        n = h1 - h0
                        ins = nc.vector.tensor_tensor(
                            m_s[:, a, h0 * KV:h1 * KV].rearrange("p (h j i) -> p h j i", j=DV, i=DH),
                            ps[:, 3 * a + g, 0:n * KV].rearrange("p (h j i) -> p h j i", j=DV, i=DH),
                            q[:, h0:h1, :].unsqueeze(2).broadcast_to([P, n, DV, DH]), ALU.mult)
                    ins.then_inc(m_done, 1)
                for a in range(TPU):
                    t = u * TPU + a
                    dve.wait_ge(m_done, t + 3)
                    nc.vector.tensor_reduce(nd[:, bass.ds(t, 1), :].rearrange("p a n -> p (a n)"),
                                            m_s[:, a].rearrange("p (n i) -> p n i", i=DH), AX.X, ALU.add).then_inc(red_done, 1)

            dve.wait_ge(phi_done, U + 2)
            units(dve, attend, 0, U // 2)

            dve.wait_ge(wall_done, 1)
            i32 = lambda a, b: sc[:, a:b].bitcast(I32)
            EXPONENT = 0x7F800000
            link(nc.vector.tensor_scalar(sc[:, 8:10], sc[:, 4:6], 1e-18, None, ALU.max))
            link(nc.vector.tensor_scalar(i32(10, 12), i32(8, 10), EXPONENT, None, ALU.bitwise_and))
            link(nc.vector.scalar_tensor_tensor(out=sc[:, 14:15], in0=sc[:, 10:11], scalar=2.0 * D, in1=sc[:, 6:7],
                                                op0=ALU.mult, op1=ALU.add))
            link(nc.vector.tensor_scalar(i32(15, 16), i32(14, 15), EXPONENT, None, ALU.bitwise_and))
            link(nc.vector.reciprocal(sc[:, 16:17], sc[:, 15:16]))
            link(nc.vector.reciprocal(sc[:, 9:10], sc[:, 11:12]))
            link(nc.vector.tensor_scalar(sc[:, 13:14], sc[:, 9:10], W_TOP, None, ALU.mult))
            link(nc.vector.tensor_scalar(sc[:, 17:18], sc[:, 16:17], H_TOP, None, ALU.mult))
            link(nc.vector.tensor_scalar(sc[:, 12:13], sc[:, 17:18], 1.0 / X_SCALE, None, ALU.mult))
            link(nc.vector.tensor_tensor(sc[:, 19:20], sc[:, 17:18], sc[:, 13:14], ALU.mult))
            nc.vector.reciprocal(sc[:, 20:21], sc[:, 19:20]).then_inc(scale_done, 1)

            units(dve, attend, U // 2, U)

            dve.wait_ge(red_done, NT + 2)
            ndv = nd[:, :, :].rearrange("p t (h j) -> p t h j", j=DV)
            link(nc.vector.tensor_scalar(rd[:, :, :], ndv[:, :, :, DH], DEN_EPS, None, ALU.add))
            link(nc.vector.reciprocal(rd[:, :, :], rd[:, :, :]))
            dve.wait_ge(xb_done, LOADS)

            def quotient(u, par):
                nc.vector.tensor_tensor(xn_s[:, par].rearrange("p a (h j) -> p a h j", j=DH),
                                        tiles(ndv, u)[:, :, :, 0:DH],
                                        tiles(rd, u).unsqueeze(3).broadcast_to([P, TPU, H, DH]), ALU.mult).then_inc(y_done, 1)

            quotient(0, 0)
            quotient(1, 1)

            def residual(it, last):
                for par in range(2):
                    u = it * 2 + par
                    dve.wait_ge(proj_done, u + 3)
                    nc.vector.tensor_tensor(tiles(x, u), ps[:, 2 + par, 0:T].rearrange("p (a d) -> p a d", a=TPU), tiles(x, u),
                                            ALU.add).then_inc(x2_done, 1)
                    if not last:
                        dve.wait_ge(yT_done, u + 1)
                        quotient(u + 2, par)
                for par in range(2):
                    u = it * 2 + par
                    dve.wait_ge(x2_done, u + 3)
                    for a in range(TPU):
                        nc.vector.bn_stats(st[:, bass.ds(u * TPU + a, 1), :].rearrange("p a s -> p (a s)"),
                                           x[:, bass.ds(u * TPU + a, 1), :].rearrange("p a d -> p (a d)")).then_inc(bn_done, 1)

            with dve.Fori(0, U // 4) as it:
                residual(it, False)
            dve.wait_ge(bn_done, NT + NT // 2)
            moments(0, NT // 2).then_inc(var2_done, 1)
            with dve.Fori(U // 4, U // 2 - 1) as it:
                residual(it, False)
            residual(U // 2 - 1, True)
            dve.wait_ge(bn_done, 2 * NT)
            moments(NT // 2, NT).then_inc(var2_done, 1)
            dve.wait_ge(var2_done, 2)

            dve.wait_ge(small_in[6], 16)
            link(nc.vector.tensor_scalar(b2s, b2r, sc[0:E, 19:20], None, ALU.mult))
            link(nc.vector.tensor_copy(b2hml[:, 0], b2s))
            link(nc.vector.tensor_tensor(b2f, b2s, b2hml[:, 0], ALU.subtract))
            link(nc.vector.tensor_copy(b2hml[:, 1], b2f))
            nc.vector.tensor_tensor(b2hml[:, 2], b2f, b2hml[:, 1], ALU.subtract).then_inc(b2_done, 1)
            dve.wait_ge(b2_done, 1)

            dve.wait_ge(rstd_done, LOADS + 1)
            norm(0, 0, 1, norm2_done)
            norm(1, 1, 1, norm2_done)
            dve.wait_ge(rstd_done, LOADS + 2)
            dve.wait_ge(small_in[4], 16)

            def route(it, last):
                for par in range(2):
                    u = it * 2 + par
                    dve.wait_ge(xh_done, u + 1)
                    nc.vector.scalar_tensor_tensor(out=x2row[:, par, :, D:2 * D], in0=xn_s[:, par], scalar=X_SCALE,
                                                   in1=x2row[:, par, :, 0:D], op0=ALU.mult,
                                                   op1=ALU.subtract).then_inc(xl_done, 1)
                    if not last:
                        dve.wait_ge(x2T_done, u + 1)
                        dve.wait_ge(xl_done, u + 1)
                        norm(u + 2, par, 1, norm2_done)
                for par in range(2):
                    u = it * 2 + par
                    dve.wait_ge(lg_done, u + 3)
                    nc.vector.tensor_tensor(tiles(lg, u), ps[:, 6 + par, 0:TPU * E].rearrange("p (a e) -> p a e", a=TPU),
                                            br[:, :].unsqueeze(1).broadcast_to([P, TPU, E]), ALU.add).then_inc(lgs_done, 1)

            with dve.Fori(0, U // 2 - 1) as it:
                route(it, False)
            route(U // 2 - 1, True)

            dve.wait_ge(lgs_done, U + 2)
            over_e = lambda a: a.unsqueeze(2).broadcast_to([P, NT, E])
            iota_t = iota[:, :].unsqueeze(1).broadcast_to([P, NT, E])

            def top(values, best, where, scratch, onehot):
                link(nc.vector.tensor_reduce(best, values, AX.X, ALU.max))
                link(nc.vector.tensor_tensor(scratch, values, over_e(best), ALU.is_equal))
                link(nc.vector.scalar_tensor_tensor(out=onehot, in0=iota_t, scalar=-float(E), in1=scratch,
                                                    op0=ALU.add, op1=ALU.mult))
                link(nc.vector.tensor_reduce(where, onehot, AX.X, ALU.min))
                link(nc.vector.tensor_scalar(where, where, float(E), None, ALU.add))
                link(nc.vector.tensor_tensor(onehot, iota_t, over_e(where), ALU.is_equal))

            top(lg[:, :, :], r1[:, 0, :], r1[:, 5, :], r8[:, 0], r8[:, 1])
            link(nc.vector.tensor_scalar(r8[:, 0], r8[:, 1], -1.0, 1.0, ALU.mult, ALU.add))
            link(nc.vector.tensor_tensor(r8[:, 2], lg[:, :, :], r8[:, 0], ALU.mult))
            link(nc.vector.scalar_tensor_tensor(out=r8[:, 2], in0=r8[:, 1], scalar=-3.4e38, in1=r8[:, 2],
                                                op0=ALU.mult, op1=ALU.add))
            top(r8[:, 2], r1[:, 1, :], r1[:, 6, :], r8[:, 0], r8[:, 3])
            nc.vector.tensor_tensor(r1[:, 3, :], r1[:, 1, :], r1[:, 0, :], ALU.subtract).then_inc(gap_done, 1)
            dve.wait_ge(gexp_done, 1)
            link(nc.vector.tensor_scalar(r1[:, 2, :], r1[:, 4, :], 1.0, None, ALU.add))
            link(nc.vector.reciprocal(r1[:, 7, :], r1[:, 2, :]))
            link(nc.vector.tensor_scalar(r1[:, 2, :], r1[:, 7, :], sc[:, 20:21], None, ALU.mult))
            link(nc.vector.tensor_tensor(r1[:, 7, :], r1[:, 2, :], r1[:, 4, :], ALU.mult))

            nc.vector.tensor_tensor(picked, r8[:, 1], r8[:, 3], ALU.add).then_inc(picked_done, 1)
            dve.wait_ge(count_done, 1)
            flat = lambda v: v.rearrange("p a b -> p (a b)")
            link(nc.vector.tensor_copy(tot, ps[:, 1, 0:NT * E].rearrange("p (t e) -> p e t", e=E)))
            dve.wait_ge(table_done, 15)
            link(nc.vector.tensor_tensor_scan(flat(upto), flat(in_round[:, :, :]), flat(tot), 0.0, ALU.mult, ALU.add))
            for r in range(R):
                nc.vector.tensor_copy(cnt[:, r, :], upto[:, :, T0[r] + RT[r] - 1]).then_inc(chain, 1)
            count["chain"] += R
            link(nc.vector.tensor_tensor(ahead, upto, tot, ALU.subtract))
            link(nc.vector.tensor_tensor(full, cnt.unsqueeze(3).broadcast_to([P, R, E, EXPERT_BLOCKS]),
                                         full_at[:, :].unsqueeze(1).unsqueeze(1).broadcast_to([P, R, E, EXPERT_BLOCKS]), ALU.is_gt))
            link(nc.vector.tensor_reduce(nblk, full, AX.X, ALU.add))
            link(nc.vector.tensor_tensor_scan(flat(ends), flat(in_row[:, :, :]), flat(nblk), 0.0, ALU.mult, ALU.add))
            link(nc.vector.tensor_tensor(base, ends, nblk, ALU.subtract))
            for r in range(R):
                link(nc.vector.tensor_scalar(base[:, r, :], base[:, r, :], float(SLOTS), float(B0[r] * SLOTS), ALU.mult, ALU.add))
            for r in range(R):
                rt = slice(T0[r], T0[r] + RT[r])
                link(nc.vector.tensor_tensor(ahead[:, :, rt], ahead[:, :, rt],
                                             base[:, r, :].unsqueeze(2).broadcast_to([P, E, RT[r]]), ALU.add))
            link(nc.vector.tensor_tensor(pos8, ps[:, 0, 0:NT * E].rearrange("p (t e) -> p t e", e=E),
                                         ahead.rearrange("p e t -> p t e"), ALU.add))
            for c, hot in enumerate((r8[:, 1], r8[:, 3])):
                link(nc.vector.tensor_tensor(r8[:, 0], hot, pos8, ALU.mult))
                link(nc.vector.tensor_reduce(pos_f[:, :, c], r8[:, 0], AX.X, ALU.add))
            link(nc.vector.tensor_copy(pos_i, pos_f))
            link(nc.vector.tensor_scalar(part_i[:, 0], pos_i, P - 1, None, ALU.bitwise_and))
            link(nc.vector.tensor_scalar(part_i[:, 1], pos_i, P.bit_length() - 1, None, ALU.logical_shift_right))
            nc.vector.tensor_copy(part_h, part_i).then_inc(part_done, 1)
            dve.wait_ge(part_done, 1)

            def slots(r):
                rt = slice(T0[r], T0[r] + RT[r])
                for c in range(TOP):
                    groups = slice(B0[r] * GPB, (B0[r] + RB[r]) * GPB)
                    nc.vector.tensor_tensor(group_eq[:, c, rt, 0:RB[r] * GPB],
                                            group_of[:, groups].unsqueeze(1).broadcast_to([P, RT[r], RB[r] * GPB]),
                                            part_h[:, 1, rt, c].unsqueeze(2).broadcast_to([P, RT[r], RB[r] * GPB]),
                                            ALU.is_equal).then_inc(group_eq_done, 1)
                    nc.vector.tensor_tensor(slot_hot[:, c, rt, :], slot_of[:, :].unsqueeze(1).broadcast_to([P, RT[r], P]),
                                            part_h[:, 0, rt, c].unsqueeze(2).broadcast_to([P, RT[r], P]),
                                            ALU.is_equal).then_inc(slot_hot_done, 1)

            def tokens(r):
                dve.wait_ge(inverse_done, r + 1)
                nc.vector.tensor_scalar(ids[:, B0[r] * GPB:(B0[r] + RB[r]) * GPB], ps[:, 7, 0:RB[r] * GPB], float(MID), None, ALU.add).then_inc(ids_done, 1)

            slots(0)
            for r in range(R):
                past = slot_past[:, 0:RB[r] * E].rearrange("p (n e) -> p n e", e=E)
                link(nc.vector.tensor_tensor(past, ends[:, r, :].unsqueeze(1).broadcast_to([P, RB[r], E]),
                                             block_f[:, 0:RB[r]].unsqueeze(2).broadcast_to([P, RB[r], E]), ALU.is_le))
                link(nc.vector.tensor_reduce(expert_f[:, B0[r]:B0[r] + RB[r]], past, AX.X, ALU.add))
            expert_b = expert_f.rearrange("p (i j) -> p i j", j=BODY)
            link(nc.vector.tensor_scalar(expert_i[:, :, 0:BODY], expert_b, float(E - 1), None, ALU.min))
            nc.vector.memset(expert_i[:, ITERS - 1, BODY:], 0).then_inc(expert_done, 1)
            nc.vector.tensor_scalar(expert_i[:, 0:ITERS - 1, BODY:], expert_b[:, 1:ITERS, 0:2], float(E - 1), None,
                                    ALU.min).then_inc(expert_done, 1)
            tokens(0)
            slots(1)
            tokens(1)
            dve.wait_ge(expert_done, 2)
            dve_experts = expert_registers(dve, "dve")

            def hidden_pre(n, j):
                dve.wait_ge(up_done, n + 3)
                dve.wait_ge(lo_done, n + 1)
                e = expert(dve, dve_experts, j)
                bank = 2 + 2 * (j % 2)
                nc.vector.tensor_tensor(pre[:, j % 2], ps[:, bank:bank + 2, :].rearrange("p b (c n) -> p (b c) n", n=SLOTS),
                                        b1s[:, bass.ds(e * HC, HC)].unsqueeze(2).broadcast_to([P, HC, SLOTS]),
                                        ALU.add).then_inc(pre_done, 1)

            def hidden_low(n, j):
                dve.wait_ge(hi_done, n + 1)
                dve.wait_ge(down_done, n + 1)
                nc.vector.scalar_tensor_tensor(out=hl[:, j], in0=pre[:, j], scalar=0.0, in1=hh[:, j],
                                               op0=ALU.max, op1=ALU.subtract).then_inc(lo_done, 1)

            def sum_y(n, it, j):
                dve.wait_ge(y_low_done, n + 1)
                dve.wait_ge(y_stored[j], it * 16 + 16)
                nc.vector.tensor_tensor(ysb[:, j], ps[:, 6 + j, :].rearrange("p (g w d) -> p g w d", g=GPB, w=2)[:, :, 0],
                                        y_low[:, j], ALU.add).then_inc(y_done2, 1)

            def mix(t, s, seen):
                dve.wait_ge(y_gathered[s], seen)
                xt = x[:, bass.ds(t, 1), :].rearrange("p a d -> p (a d)")
                nc.vector.scalar_tensor_tensor(out=xt, in0=yg[:, s, 0], scalar=r1[:, 2, bass.ds(t, 1)], in1=xt,
                                               op0=ALU.mult, op1=ALU.add).then_inc(mix_half, 1)
                dve.wait_ge(mix_half, t + 1)
                nc.vector.scalar_tensor_tensor(out=xt, in0=yg[:, s, 1], scalar=r1[:, 7, bass.ds(t, 1)], in1=xt,
                                               op0=ALU.mult, op1=ALU.add).then_inc(mix_done, 1)

            def dve_steps(it):
                load_experts(dve, dve_experts, it)
                for j in range(BODY):
                    n = it * BODY + j
                    if exists(n + 1):
                        hidden_pre(n + 1, j + 1)
                    hidden_low(n, j)
                    if j:
                        sum_y(n - 1, it, j - 1)
                    elif not isinstance(it, int) or it:
                        sum_y(n - 1, it - 1, BODY - 1)

            def dve_pair(q):
                for half in range(2):
                    dve_steps(q * 2 + (MIX_FROM + half))
                    for s in range(half * MIX, half * MIX + MIX):
                        mix(q * (2 * MIX) + s, s, q * (16 * TOP) + 16 * TOP)

            load_experts(dve, dve_experts, 0)
            hidden_pre(0, 0)
            dve_steps(0)
            with dve.Fori(1, MIX_FROM) as it:
                dve_steps(it)
            with dve.Fori(0, PAIRS - 1) as q:
                dve_pair(q)
            dve_pair(PAIRS - 1)
            sum_y(NBLK - 1, ITERS - 1, BODY - 1)
            for s in range(2 * MIX):
                mix(PAIRS * 2 * MIX + s, s, (PAIRS + 1) * 16 * TOP)
            with dve.Fori(0, RT[1] // TAIL) as it:
                for s in range(TAIL):
                    slot = (s + 2 * MIX) % TAIL
                    before = PAIRS + 1 if slot < 2 * MIX else 0
                    mix(it * TAIL + (T0[1] + s), slot, it * (16 * TOP) + (before + 1) * 16 * TOP)

        @block.tensor
        def _(pe):
            pe.wait_ge(const_done, 6)

            def turn(bank, par, done):
                for a in range(TPU):
                    ins = nc.tensor.transpose(ps[:, bank, a * P:(a + 1) * P], xn_s[:, par, a], ident[:, :])
                ins.then_inc(done, 1)

            def turn_x(u, par):
                pe.wait_ge(norm_done, u + 1)
                turn(par, par, xT_done)

            turn_x(0, 0)
            turn_x(1, 1)
            pe.wait_ge(wq_in, 16)

            def qkv(it, last):
                for par in range(2):
                    u = it * 2 + par
                    pe.wait_ge(xT_out, u + 1)
                    pe.wait_ge(qkv_free, u * 2 + 2)
                    for a in range(TPU):
                        ins = nc.tensor.matmul(ps[:, 2 + 2 * par + a, 0:3 * D], xT_s[:, par, a * P:(a + 1) * P], wqkv[:, :],
                                               start=True, stop=True)
                    ins.then_inc(qkv_done, 1)
                if not last:
                    for par in range(2):
                        turn_x(it * 2 + par + 2, par)

            with pe.Fori(0, U // 2 - 1) as it:
                qkv(it, False)
            qkv(U // 2 - 1, True)

            pe.wait_ge(small_in[5], 16)
            nc.tensor.transpose(ps[:, 6, 0:E * HC], b1r[:, :], ident[0:E * HC, 0:E * HC]).then_inc(b1T_done, 1)

            pe.wait_ge(qkv_free, 2 * U + 4)

            def prefix(u, par):
                for a in range(TPU):
                    pe.wait_ge(kv_done, u * TPU + (a + 1))
                    pe.wait_ge(m_done, u * TPU + (a + 1))
                    for g, (h0, h1) in enumerate(HEADS):
                        o = ps[:, 3 * a + g, 0:(h1 - h0) * KV]
                        kv = [kv_s[:, par, b, h0:h1, :].rearrange("p h n -> p (h n)") for b in range(TPU)]
                        if a == 1:
                            nc.tensor.matmul(o, ones[:, :], kv[0], start=True, stop=False)
                        ins = nc.tensor.matmul(o, tri[:, :], kv[a], start=(a == 0), stop=True)
                    ins.then_inc(pfx_done, 1)

            units(pe, prefix, 0, U)

            def turn_y(u, par):
                pe.wait_ge(y_done, u + 1)
                turn(par, par, yT_done)

            turn_y(0, 0)
            turn_y(1, 1)
            pe.wait_ge(small_in[2], 16)

            def proj(it, last):
                for par in range(2):
                    u = it * 2 + par
                    pe.wait_ge(yT_out, u + 1)
                    pe.wait_ge(x2_done, u + 1)
                    for a in range(TPU):
                        ins = nc.tensor.matmul(ps[:, 2 + par, a * P:(a + 1) * P], xT_s[:, par, a * P:(a + 1) * P], wproj[:, :],
                                               start=True, stop=True)
                    ins.then_inc(proj_done, 1)
                if not last:
                    for par in range(2):
                        turn_y(it * 2 + par + 2, par)

            with pe.Fori(0, U // 2 - 1) as it:
                proj(it, False)
            proj(U // 2 - 1, True)

            def turn_x2(u, par):
                pe.wait_ge(norm2_done, u + 1)
                turn(4 + par, par, x2T_done)

            turn_x2(0, 0)
            turn_x2(1, 1)
            pe.wait_ge(small_in[3], 16)

            def router(it, last):
                for par in range(2):
                    u = it * 2 + par
                    pe.wait_ge(x2T_out, u + 1)
                    pe.wait_ge(lgs_done, u + 1)
                    for a in range(TPU):
                        ins = nc.tensor.matmul(ps[:, 6 + par, a * E:(a + 1) * E], xT_s[:, par, a * P:(a + 1) * P], wr[:, :],
                                               start=True, stop=True)
                    ins.then_inc(lg_done, 1)
                if not last:
                    for par in range(2):
                        turn_x2(it * 2 + par + 2, par)

            with pe.Fori(0, U // 2 - 1) as it:
                router(it, False)
            router(U // 2 - 1, True)

            pe.wait_ge(table_done, 15)
            pe.wait_ge(picked_done, 1)
            nc.tensor.matmul(ps[:, 0, 0:NT * E], before_h[:, :], picked.rearrange("p t e -> p (t e)"), start=True, stop=True)
            nc.tensor.matmul(ps[:, 1, 0:NT * E], ones_h[:, :], picked.rearrange("p t e -> p (t e)"),
                             start=True, stop=True).then_inc(count_done, 1)

            for r in range(R):
                if r:
                    pe.wait_ge(ids_done, r)
                for c in range(TOP):
                    pe.wait_ge(slot_hot_done, r * TOP + (c + 1))
                    pe.wait_ge(group_hot_done, r * TOP + (c + 1))
                    for t in range(T0[r], T0[r] + RT[r]):
                        first, last = t == T0[r] and c == 0, t == T0[r] + RT[r] - 1 and c == TOP - 1
                        ins = nc.tensor.matmul(ps[:, 7, 0:RB[r] * GPB], slot_hot[:, c, t, :], group_hot[:, c, t, 0:RB[r] * GPB],
                                               start=first, stop=last)
                ins.then_inc(inverse_done, 1)

            pe.wait_ge(wlo_done, 2)
            pe.wait_ge(b2_in, 32)
            pe.wait_ge(expert_done, 2)
            pe_experts = expert_registers(pe, "pe")

            def turn_block(it, j):
                pe.wait_ge(gathered[j % 2], (it + j // BODY) * (16 * GPB) + 16 * GPB)
                pe.wait_ge(turn_out, it * BODY + (j + 1))
                for g in range(GPB):
                    for w in range(2):
                        at = w * SLOTS + g * P
                        ins = nc.tensor.matmul(ps[:, j % 2, at:at + P], xg[:, j % 2, g, w], ident_h[:, :], start=True, stop=True)
                ins.then_inc(turn_done, 1)

            def up(n, j):
                e = expert(pe, pe_experts, j)
                pe.wait_ge(turn_out, n + 3)
                pe.wait_ge(pre_done, n + 1)
                xh, xl = xgT[:, j % 2, 0], xgT[:, j % 2, 1]
                for c in range(HC):
                    col = c % 2 * SLOTS
                    o = ps[:, 2 + 2 * (j % 2) + c // 2, col:col + SLOTS]
                    wh, wl = (w[:, bass.ds(e, 1), c * P:(c + 1) * P].rearrange("p a h -> p (a h)") for w in (w1h, w1l))
                    nc.tensor.matmul(o, wh, xh, start=True, stop=False)
                    nc.tensor.matmul(o, wh, xl, start=False, stop=False)
                    ins = nc.tensor.matmul(o, wl, xh, start=False, stop=True)
                ins.then_inc(up_done, 1)

            def down(n, j):
                e = expert(pe, pe_experts, j)
                pe.wait_ge(y_done2, n + 1)
                pe.wait_ge(lo_done, n + 3)
                rows = [ps[:, 6 + j, g * 2 * D:(g + 1) * 2 * D] for g in range(GPB)]
                for c in range(HC):
                    wc = w2[:, bass.ds(e, 1), c].rearrange("p a w d -> p (a w d)")
                    wh = w2[:, bass.ds(e, 1), c, 0].rearrange("p a d -> p (a d)")
                    for g, o in enumerate(rows):
                        slots_g = slice(g * P, (g + 1) * P)
                        nc.tensor.matmul(o, hh[:, j, c, slots_g], wc, start=(c == 0 and g == 0), stop=False)
                        nc.tensor.matmul(o[:, 0:D], hl[:, j, c, slots_g], wh, start=False, stop=False)
                for g, o in enumerate(rows):
                    ins = nc.tensor.matmul(o[:, 0:D], ones3[:, :], b2p[:, bass.ds(e, 1), :].rearrange("p a d -> p (a d)"),
                                           start=False, stop=(g == GPB - 1))
                ins.then_inc(down_done, 1)

            def pe_steps(it):
                load_experts(pe, pe_experts, it)
                for j in range(BODY):
                    n = it * BODY + j
                    if exists(n + 2):
                        up(n + 2, j + 2)
                    down(n, j)
                    if exists(n + 4):
                        turn_block(it, j + 4)

            load_experts(pe, pe_experts, 0)
            turn_block(0, 0)
            turn_block(0, 1)
            up(0, 0)
            turn_block(0, 2)
            up(1, 1)
            turn_block(0, 3)
            with pe.Fori(0, ITERS - 2) as it:
                pe_steps(it)
            pe_steps(ITERS - 2)
            pe_steps(ITERS - 1)


_INS = ['L0_attn_x', 'L0_attn_W_attn', 'L0_attn_b_attn', 'L0_attn_W_proj', 'L0_attn_b_proj', 'L0_ffn_W1', 'L0_ffn_b1',
        'L0_ffn_W2', 'L0_ffn_b2', 'L0_ffn_Wr', 'L0_ffn_br']


def kernel(**inputs):
    import numpy as _np
    import concourse.bacc as _bacc
    from concourse import mybir as _mybir
    from concourse.bass_utils import run_bass_kernel_spmd as _run

    nc = _bacc.Bacc("TRN2", target_bir_lowering=False, num_devices=1)
    arrays, args = {}, []
    for name in _INS:
        a = _np.ascontiguousarray(inputs[name])
        arrays[f"in_{name}_dram"] = a
        args.append(nc.dram_tensor(f"in_{name}_dram", a.shape, _mybir.dt.from_np(a.dtype), kind="ExternalInput").ap())
    out = nc.dram_tensor("out_dram", inputs['L0_attn_x'].shape, F32, kind="ExternalOutput").ap()
    block_kernel(nc, *args, out)
    r = _run(nc, [arrays], core_ids=[0])
    return r.results[0]["out_dram"]
```

```python
from contextlib import ExitStack

import concourse.bass as bass
from concourse import mybir

F32 = mybir.dt.float32
F16 = mybir.dt.float16
BF16 = mybir.dt.bfloat16
I32 = mybir.dt.int32
ALU = mybir.AluOpType
ACT = mybir.ActivationFunctionType
AX = mybir.AxisListType


def block_kernel(nc, x_d, wqkv_d, bqkv_d, wproj_d, bproj_d, w1_d, b1_d, w2_d, b2_d, wr_d, br_d, out_d):
    P = 128
    SEQS, T, D = x_d.shape
    NT = SEQS * T // P
    U = SEQS
    TPU = T // P
    H, DH = 16, D // 16
    E, _, HID = w1_d.shape
    HC = HID // P
    DV = DH + 1
    KV = DV * DH
    LN_EPS, DEN_EPS = 1e-5, 1e-6
    LOADS = 4
    TPL = NT // LOADS
    assert TPU == 2 and D == P and U % 4 == 0

    HEADS = [(0, 6), (6, 11), (11, 16)]
    X_SCALE = 2.0 ** 4
    W_TOP = 2.0 ** 9
    H_TOP = 2.0 ** 14
    TOP = 2
    GPB = 2
    SLOTS = GPB * P
    RT = [22, NT - 22]
    R = len(RT)
    T0 = [sum(RT[:r]) for r in range(R)]
    RB = [TOP * n // GPB + E - 1 for n in RT]
    B0 = [sum(RB[:r]) for r in range(R)]
    NBLK = sum(RB)
    EXPERT_BLOCKS = -(-max(RT) * P // SLOTS)
    BODY = 2
    ITERS = NBLK // BODY
    PE_PASSES = 3
    GATHERS = 8
    MID = NT * P // 2
    assert NBLK % BODY == 0 and (ITERS - 2) % PE_PASSES == 0 and RT[0] % 2 == 0

    xv = x_d.rearrange("s (a p) d -> p (s a) d", p=P)
    ov = out_d.rearrange("s (a p) d -> p (s a) d", p=P)

    x2_rows = nc.dram_tensor("x2_rows", [NT * P, D], F32).ap()
    y_rows = nc.dram_tensor("y_rows", [NBLK * SLOTS, D], F32).ap()
    b2_parts = nc.dram_tensor("b2_parts", [3, E, D], BF16).ap()
    yv = y_rows.rearrange("(b g p) d -> p b g d", g=GPB, p=P)
    x2v = x2_rows.rearrange("(t p) c -> p t c", p=P)

    with ExitStack() as ctx:
        def sb(name, shape, dt=F32):
            return ctx.enter_context(nc.sbuf_tensor(name, shape, dt))

        def sem(name):
            return ctx.enter_context(nc.semaphore(name))

        ps = ctx.enter_context(nc.psum_tensor("ps", [P, 8, 512], F32))

        x = sb("x", [P, NT, D])
        wqkv = sb("wqkv", [P, 3 * D])
        bqkv = sb("bqkv", [P, 3 * D])
        wproj = sb("wproj", [P, D])
        bproj = sb("bproj", [P, D])
        wr = sb("wr", [P, E])
        wr_rest = sb("wr_rest", [P, E])
        wr_parts = sb("wr_parts", [P, 3, E], BF16)
        br = sb("br", [P, E])
        w1h = sb("w1h", [P, E, HID], F16)
        w1l = sb("w1l", [P, E, HID], F16)
        w2 = sb("w2", [P, E, HC, 2, D], F16)
        big = sb("big", [P, 2 * E * HID + 2 * TPU * H * KV])
        b1r = sb("b1r", [E * HC, P])
        b1T = sb("b1T", [P, E * HC])
        b1s = sb("b1s", [P, E * HC])
        b2p = sb("b2p", [3, E, D], BF16)
        ones3 = sb("ones3", [3, P], BF16)
        ident = sb("ident", [P, P])
        tri = sb("tri", [P, P])
        ones = sb("ones", [P, P])
        neghalf = sb("neghalf", [P, NT])
        iota_i = sb("iota_i", [P, E], I32)
        iota = sb("iota", [P, E])
        st = sb("st", [P, NT, 6])
        lnt = sb("lnt", [P, 7, NT])
        rstd = sb("rstd", [P, 2, NT])
        xn_s = sb("xn_s", [P, 2, TPU, D])
        xT_s = sb("xT_s", [P, 2, T])
        work = sb("work", [P, 2 * H * KV])
        qk = sb("qk", [P, NT, 2 * D])
        vaug = sb("vaug", [P, NT, H, DV])
        nd = sb("nd", [P, NT, H * DV])
        rd = sb("rd", [P, 2, TPU, H])
        lg = sb("lg", [P, NT, E])
        r8 = sb("r8", [P, 4, NT, E])
        r1 = sb("r1", [P, 8, NT])
        ident_h = sb("ident_h", [P, P], F16)
        ones_h = sb("ones_h", [P, P], F16)
        before_h = sb("before_h", [P, P], F16)
        count_i = sb("count_i", [P, P], I32)
        slot_of = sb("slot_of", [P, P], F16)
        group_of = sb("group_of", [P, NBLK * GPB], F16)
        block_f = sb("block_f", [P, NBLK])
        full_at = sb("full_at", [P, EXPERT_BLOCKS])
        token_of = sb("token_of", [P, NT], F16)
        in_round = sb("in_round", [P, E, NT])
        in_row = sb("in_row", [P, R, E])
        b2hml = sb("b2hml", [E, 3, D], BF16)
        sc = sb("sc", [P, 24])
        ndv = nd[:, :, :].rearrange("p t (h j) -> p t h j", j=DV)
        ndf = nd[:, :, :].rearrange("p t n -> p (t n)")
        wf = big[:, 0:2 * E * HID].rearrange("p (w n) -> p w n", w=2)
        kvf = big[:, 2 * E * HID:]
        kv_s = kvf.rearrange("p (b a h n) -> p b a h n", b=2, a=TPU, h=H)
        x2_words = kvf[:, 4 * D:4 * D + NT * D].rearrange("p (t d) -> p t d", t=NT)
        x2row = kvf[:, 4 * D:4 * D + NT * D].bitcast(F16).rearrange("p (t c) -> p t c", t=NT)
        xg_words = big[:, 0:NBLK * GPB * D].rearrange("p (b n) -> p b n", b=NBLK)
        xg = big[:, 0:NBLK * GPB * D].bitcast(F16).rearrange("p (b g w d) -> p b g w d", b=NBLK, g=GPB, w=2)
        w2p = w2[:, :, :, :, :].rearrange("p e c w d -> p (e c) w d")
        wf2 = wf[:, 1].rearrange("p (n d) -> p n d", d=D)
        b2r, b2s, b2f = (kvf[0:E, n * D:(n + 1) * D] for n in range(3))
        te = work[:, 0:4 * T * 2].rearrange("p (w a t d) -> p w a t d", w=2, a=2, t=TPU)
        t_s, e_s = te[:, 0], te[:, 1]
        m_s = work[:, :].rearrange("p (a n) -> p a n", a=2)

        def places(region):
            at = [0]

            def place(n, dt=F32):
                words = n if dt in (F32, I32) else n // 2
                at[0] += words
                assert at[0] <= region.shape[1]
                v = region[:, at[0] - words:at[0]]
                return v if dt == F32 else v.bitcast(dt)
            return place

        qkf = qk[:, :, :].rearrange("p t d -> p (t d)")
        yg = qkf[:, 0:NT * TOP * D].rearrange("p (t c d) -> p t c d", t=NT, c=TOP)
        in_qk = places(qkf)
        slot_hot = in_qk(TOP * NT * P, F16).rearrange("p (c t s) -> p c t s", c=TOP, t=NT)
        HG = RB[0] * GPB
        group_hot = in_qk(TOP * NT * HG, F16).rearrange("p (c t n) -> p c t n", c=TOP, t=NT)
        in_nd = places(ndf)
        pre = in_nd(2 * HC * SLOTS).rearrange("p (b c n) -> p b c n", b=2, c=HC)
        hh = in_nd(2 * HC * SLOTS, F16).rearrange("p (b c n) -> p b c n", b=2, c=HC)
        hl = in_nd(2 * HC * SLOTS, F16).rearrange("p (b c n) -> p b c n", b=2, c=HC)
        x2T = xT_s[:, :, :].bitcast(F16)
        in_work = places(work[:, :])
        xgT = in_work(2 * 2 * SLOTS, F16).rearrange("p (b w n) -> p b w n", b=2, w=2)
        y_low = in_work(2 * GPB * D).rearrange("p (b g d) -> p b g d", b=2, g=GPB)
        in_v = places(vaug[:, :, :, :].rearrange("p t h d -> p (t h d)"))
        ysb = in_v(2 * GPB * D).rearrange("p (b g d) -> p b g d", b=2, g=GPB)
        group_eq = in_v(TOP * RT[0] * HG, F16).rearrange("p (c t n) -> p c t n", c=TOP, t=RT[0])
        ids = in_v(NBLK * GPB, I32)
        expert_i = in_v(ITERS * (BODY + 2), I32).rearrange("p (i j) -> p i j", j=BODY + 2)
        pos_i = in_v(NT * TOP, I32).rearrange("p (t c) -> p t c", c=TOP)
        part_i = in_v(2 * NT * TOP, I32).rearrange("p (w t c) -> p w t c", w=2, c=TOP)
        part_h = in_v(2 * NT * TOP, F16).rearrange("p (w t c) -> p w t c", w=2, c=TOP)
        pos_f = in_v(NT * TOP).rearrange("p (t c) -> p t c", c=TOP)
        picked = in_v(NT * E, F16).rearrange("p (t e) -> p t e", e=E)
        tot, upto, ahead = (in_v(E * NT).rearrange("p (e t) -> p e t", e=E) for _ in range(3))
        pos8 = in_v(NT * E).rearrange("p (t e) -> p t e", e=E)
        cnt, nblk, ends, base = (in_v(R * E).rearrange("p (r e) -> p r e", r=R) for _ in range(4))
        full = in_v(R * E * EXPERT_BLOCKS).rearrange("p (r e j) -> p r e j", r=R, e=E)
        slot_past = in_work(RB[0] * E)
        expert_f = in_work(NBLK)

        x_in = [sem(f"x_in{g}") for g in range(LOADS)]
        wq_in = sem("wq_in")
        w1_in = sem("w1_in")
        w2_in = sem("w2_in")
        small_in = [sem(f"small_in{g}") for g in range(7)]
        const_done = sem("const_done")
        table_done = sem("table_done")
        chain = sem("chain")
        pchain = sem("pchain")
        achain = sem("achain")
        stats_done = sem("stats_done")
        rstd_done = sem("rstd_done")
        bn_done = sem("bn_done")
        norm_done = sem("norm_done")
        xT_done = sem("xT_done")
        xT_out = sem("xT_out")
        qkv_done = sem("qkv_done")
        qkv_free = sem("qkv_free")
        t_done = sem("t_done")
        relu_done = sem("relu_done")
        exp_done = sem("exp_done")
        phi_done = sem("phi_done")
        kv_done = sem("kv_done")
        pfx_done = sem("pfx_done")
        m_done = sem("m_done")
        red_done = sem("red_done")
        xb_done = sem("xb_done")
        den_done = sem("den_done")
        rd_done = sem("rd_done")
        y_done = sem("y_done")
        yT_done = sem("yT_done")
        yT_out = sem("yT_out")
        proj_done = sem("proj_done")
        x2_done = sem("x2_done")
        var2_done = sem("var2_done")
        norm2_done = sem("norm2_done")
        x2T_done = sem("x2T_done")
        x2T_out = sem("x2T_out")
        lg_done = sem("lg_done")
        lgs_done = sem("lgs_done")
        wr_done = sem("wr_done")
        gap_done = sem("gap_done")
        gexp_done = sem("gexp_done")
        b1T_done = sem("b1T_done")
        b1T_out = sem("b1T_out")
        wmax_done = sem("wmax_done")
        wall_done = sem("wall_done")
        scale_done = sem("scale_done")
        whi_done = sem("whi_done")
        wscaled_done = sem("wscaled_done")
        wlo_done = sem("wlo_done")
        b2_done = sem("b2_done")
        b2_in = sem("b2_in")
        out_done = sem("out_done")
        xh_done = sem("xh_done")
        xl_done = sem("xl_done")
        x2_stored = sem("x2_stored")
        picked_done = sem("picked_done")
        count_done = sem("count_done")
        part_done = sem("part_done")
        slot_hot_done = sem("slot_hot_done")
        group_eq_done = sem("group_eq_done")
        group_hot_done = sem("group_hot_done")
        inverse_done = sem("inverse_done")
        ids_done = sem("ids_done")
        expert_done = sem("expert_done")
        gathered = [sem(f"gathered{b}") for b in range(2)]
        turn_done = sem("turn_done")
        turn_out = sem("turn_out")
        up_done = sem("up_done")
        pre_done = sem("pre_done")
        hi_done = sem("hi_done")
        lo_done = sem("lo_done")
        down_done = sem("down_done")
        y_low_done = sem("y_low_done")
        y_sum_done = sem("y_sum_done")
        y_stored = [sem(f"y_stored{b}") for b in range(2)]
        y_gathered = [sem(f"y_gathered{b}") for b in range(GATHERS)]
        mix_half = sem("mix_half")
        mix_done = sem("mix_done")

        block = ctx.enter_context(nc.Block())

        def stored_before(n, b):
            return len(range(b, n, 2))

        def units(eng, body, first, end):
            with eng.Fori(first // 2, end // 2) as it:
                for par in range(2):
                    body(it * 2 + par, par)

        def exists(n):
            return not isinstance(n, int) or n < NBLK

        def expert_registers(eng, which, passes=1):
            return [eng.alloc_register(name=f"{which}_expert{j}") for j in range(passes * (BODY + 2))]

        def load_experts(eng, regs, it):
            eng.load(regs, expert_i[0:1, bass.ds(it, len(regs) // (BODY + 2)), :].rearrange("p a j -> p (a j)"))

        def expert(eng, regs, j):
            return eng.snap(regs[j], min_val=0, max_val=E - 1)

        def tiles(t, u):
            return t[:, bass.ds(u * TPU, TPU)]

        @block.sync
        def _(sp):
            for g in range(LOADS):
                sp.dma_start(x[:, g * TPL:(g + 1) * TPL, :], xv[:, g * TPL:(g + 1) * TPL, :]).then_inc(x_in[g], 16)
            sp.dma_start(wf[:, 0, :].rearrange("p (e h) -> p e h", e=E), w1_d.rearrange("e d h -> d e h")).then_inc(w1_in, 16)
            sp.dma_start(wf[:, 1, :].rearrange("p (e c d) -> p e c d", e=E, c=HC),
                         w2_d.rearrange("e (c p) d -> p e c d", p=P)).then_inc(w2_in, 16)
            sp.wait_ge(pfx_done, NT + 2 * TPU)
            sp.dma_start(b2r, b2_d).then_inc(small_in[6], 16)
            sp.wait_ge(b2_done, 1)
            sp.dma_start(b2_parts.rearrange("r e d -> e r d"), b2hml[:, :, :]).then_inc(b2_in, 16)
            sp.wait_ge(b2_in, 16)
            sp.dma_start(b2p[:, :, :], b2_parts).then_inc(b2_in, 16)

            def store_x2(u, par):
                sp.wait_ge(xl_done, u + 1)
                sp.dma_start(tiles(x2v, u), tiles(x2_words, u)).then_inc(x2_stored, 16)

            units(sp, store_x2, 0, U)

            def store_y(n, j):
                sp.wait_ge(y_sum_done, n + 3)
                sp.dma_start(yv[:, bass.ds(n, 1)].rearrange("p a g d -> p (a g) d"), ysb[:, j]).then_inc(y_stored[j], 16)

            def store_out(t, n):
                sp.wait_ge(mix_done, t + n)
                sp.dma_start(ov[:, bass.ds(t, n), :], x[:, bass.ds(t, n), :]).then_inc(out_done, 16)

            with sp.Fori(0, ITERS) as it:
                for j in range(BODY):
                    store_y(it * BODY + j, j)
            for t in range(0, T0[1], 2):
                store_out(t, 2)
            with sp.Fori(T0[1], NT) as t:
                store_out(t, 1)
            sp.wait_ge(out_done, 16 * (T0[1] // 2 + RT[1]))

        @block.gpsimd
        def _(pool):
            nc.gpsimd.memset(ident[:], 0.0).then_inc(pchain, 1)
            nc.gpsimd.memset(ones[:], 1.0).then_inc(pchain, 1)
            nc.gpsimd.memset(ones3[:], 1.0).then_inc(const_done, 1)
            nc.gpsimd.memset(neghalf[:], -0.5).then_inc(const_done, 1)
            nc.gpsimd.memset(vaug[:, :, :, DH:DV], 1.0).then_inc(const_done, 1)
            nc.gpsimd.iota(iota_i[:], [[1, E]], base=0, channel_multiplier=0).then_inc(pchain, 1)
            pool.wait_ge(pchain, 3)
            nc.gpsimd.affine_select(out=ident[:], in_=ident[:], compare_op=ALU.not_equal, fill=1.0, base=0,
                                    pattern=[[-1, P]], channel_multiplier=1).then_inc(const_done, 1)
            nc.gpsimd.affine_select(out=tri[:], in_=ones[:], compare_op=ALU.is_ge, fill=0.0, base=0,
                                    pattern=[[1, P]], channel_multiplier=-1).then_inc(const_done, 1)
            nc.gpsimd.tensor_copy(iota[:], iota_i[:]).then_inc(const_done, 1)

            nc.gpsimd.memset(ones_h[:], 1.0).then_inc(table_done, 1)
            nc.gpsimd.memset(in_round[:], 1.0).then_inc(table_done, 1)
            nc.gpsimd.memset(in_row[:], 1.0).then_inc(table_done, 1)
            nc.gpsimd.iota(count_i[:], [[1, P]], base=0, channel_multiplier=0).then_inc(table_done, 1)
            pool.wait_ge(const_done, 6)
            pool.wait_ge(table_done, 4)
            nc.gpsimd.tensor_copy(ident_h[:], ident[:]).then_inc(table_done, 1)
            nc.gpsimd.affine_select(out=before_h[:], in_=ones_h[:], compare_op=ALU.is_ge, fill=0.0, base=-1,
                                    pattern=[[1, P]], channel_multiplier=-1).then_inc(table_done, 1)
            for r in range(R):
                nc.gpsimd.memset(in_round[:, :, T0[r]:T0[r] + 1], 0.0).then_inc(table_done, 1)
            nc.gpsimd.memset(in_row[:, :, 0:1], 0.0).then_inc(table_done, 1)
            nc.gpsimd.tensor_copy(slot_of[:], count_i[:]).then_inc(table_done, 1)
            nc.gpsimd.tensor_copy(group_of[:], count_i[:, 0:NBLK * GPB]).then_inc(table_done, 1)
            nc.gpsimd.tensor_copy(block_f[:], count_i[:, 0:NBLK]).then_inc(table_done, 1)
            nc.gpsimd.tensor_scalar(full_at[:], count_i[:, 0:EXPERT_BLOCKS], float(SLOTS), None, ALU.mult).then_inc(table_done, 1)
            pool.wait_ge(table_done, 13)
            nc.gpsimd.iota(count_i[:, 0:NT], [[P, NT]], base=-MID, channel_multiplier=1).then_inc(table_done, 1)
            pool.wait_ge(table_done, 14)
            nc.gpsimd.tensor_copy(token_of[:], count_i[:, 0:NT]).then_inc(table_done, 1)

            pool.wait_ge(const_done, 6)
            for g in range(LOADS):
                gt = slice(g * TPL, (g + 1) * TPL)
                pool.wait_ge(stats_done, g + 1)
                nc.gpsimd.tensor_tensor(rstd[:, 0, gt], lnt[:, 4, gt], neghalf[:, gt], ALU.pow).then_inc(rstd_done, 1)

            pool.wait_ge(small_in[1], 16)
            for g in range(LOADS):
                xg_in = x[:, g * TPL:(g + 1) * TPL, :]
                pool.wait_ge(norm_done, (g + 1) * TPL // TPU)
                nc.gpsimd.tensor_tensor(xg_in, xg_in, bproj[:, :].unsqueeze(1).broadcast_to([P, TPL, D]), ALU.add).then_inc(xb_done, 1)

            pool.wait_ge(small_in[3], 16)
            nc.gpsimd.tensor_copy(wr_parts[:, 0], wr[:, :]).then_inc(wr_done, 1)
            pool.wait_ge(wr_done, 1)
            nc.gpsimd.tensor_tensor(wr_rest[:, :], wr[:, :], wr_parts[:, 0], ALU.subtract).then_inc(wr_done, 1)
            pool.wait_ge(wr_done, 2)
            nc.gpsimd.tensor_copy(wr_parts[:, 1], wr_rest[:, :]).then_inc(wr_done, 1)
            pool.wait_ge(wr_done, 3)
            nc.gpsimd.tensor_tensor(wr_parts[:, 2], wr_rest[:, :], wr_parts[:, 1], ALU.subtract).then_inc(wr_done, 1)

            def kv_products(u, par):
                pool.wait_ge(phi_done, u + 3)
                pool.wait_ge(pfx_done, u * 2 + 2)
                for a in range(TPU):
                    k = qk[:, bass.ds(u * TPU + a, 1), D:2 * D].rearrange("p a (h i) -> p (a h) i", i=DH)
                    v = vaug[:, bass.ds(u * TPU + a, 1), :, :].rearrange("p a h j -> p (a h) j")
                    nc.gpsimd.tensor_tensor(kv_s[:, par, a].rearrange("p h (j i) -> p h j i", j=DV),
                                            k.unsqueeze(2).broadcast_to([P, H, DV, DH]),
                                            v.unsqueeze(3).broadcast_to([P, H, DV, DH]), ALU.mult).then_inc(kv_done, 1)

            def quotient(u, par):
                pool.wait_ge(rd_done, u + 1)
                nc.gpsimd.tensor_tensor(xn_s[:, par].rearrange("p a (h j) -> p a h j", j=DH),
                                        tiles(ndv, u)[:, :, :, 0:DH],
                                        rd[:, par].unsqueeze(3).broadcast_to([P, TPU, H, DH]), ALU.mult).then_inc(y_done, 1)

            def products_and_quotient(u, par):
                kv_products(u, par)
                quotient(u - 2, par)

            units(pool, kv_products, 0, 2)
            units(pool, products_and_quotient, 2, U // 4)
            pool.wait_ge(wmax_done, 3)
            nc.gpsimd.partition_all_reduce(sc[:, 4:7], sc[:, 0:3], P, bass.bass_isa.ReduceOp.max).then_inc(wall_done, 1)
            units(pool, products_and_quotient, U // 4, U)
            quotient(U - 2, 0)
            quotient(U - 1, 1)
            for half in range(2):
                ht = slice(half * NT // 2, (half + 1) * NT // 2)
                pool.wait_ge(var2_done, half + 1)
                nc.gpsimd.tensor_tensor(rstd[:, 1, ht], lnt[:, 4, ht], neghalf[:, ht], ALU.pow).then_inc(rstd_done, 1)

            pool.wait_ge(whi_done, 2 * E)
            for w in range(2):
                nc.gpsimd.tensor_scalar(wf[:, w], wf[:, w], sc[:, 12 + w:13 + w], None, ALU.mult).then_inc(wscaled_done, 1)
            pool.wait_ge(wscaled_done, 2)
            nc.gpsimd.tensor_tensor(w1l[:].rearrange("p e h -> p (e h)"), wf[:, 0], w1h[:].rearrange("p e h -> p (e h)"),
                                    ALU.subtract).then_inc(wlo_done, 1)
            nc.gpsimd.tensor_tensor(w2p[:, :, 1], wf2, w2p[:, :, 0], ALU.subtract).then_inc(wlo_done, 1)

            def gather_x(n):
                if n >= 2:
                    pool.wait_ge(gathered[n % 2], 16 * GPB * (n // 2))
                for g in range(GPB):
                    col = n * GPB + g
                    nc.gpsimd.indirect_dma_start(out=xg_words[:, n, g * D:(g + 1) * D], out_offset=None, in_=x2_rows,
                                                 in_offset=bass.IndirectOffsetOnAxis(ap=ids[:, col:col + 1], axis=0)
                                                 ).then_inc(gathered[n % 2], 16)

            def gather_y(t, rows):
                if t >= GATHERS:
                    pool.wait_ge(y_gathered[t % GATHERS], 16 * TOP * (t // GATHERS))
                for c in range(TOP):
                    nc.gpsimd.indirect_dma_start(out=yg[:, t, c], out_offset=None, in_=rows,
                                                 in_offset=bass.IndirectOffsetOnAxis(ap=pos_i[:, t, c:c + 1], axis=0)
                                                 ).then_inc(y_gathered[t % GATHERS], 16)

            def group_tokens(r):
                rt = slice(T0[r], T0[r] + RT[r])
                for c in range(TOP):
                    pool.wait_ge(group_eq_done, r * TOP + (c + 1))
                    nc.gpsimd.tensor_tensor(group_hot[:, c, rt, 0:RB[r] * GPB], group_eq[:, c, 0:RT[r], 0:RB[r] * GPB],
                                            token_of[:, rt].unsqueeze(2).broadcast_to([P, RT[r], RB[r] * GPB]),
                                            ALU.mult).then_inc(group_hot_done, 1)

            group_tokens(0)
            pool.wait_ge(x2_stored, 16 * U)
            pool.wait_ge(wlo_done, 2)
            pool.wait_ge(ids_done, 1)
            gather_x(0)
            group_tokens(1)
            for n in range(1, NBLK):
                if n == B0[1]:
                    pool.wait_ge(ids_done, 2)
                gather_x(n)
            for r in range(R):
                for b in range(2):
                    pool.wait_ge(y_stored[b], 16 * (1 + stored_before(B0[r] + RB[r], b)))
                for t in range(T0[r], T0[r] + RT[r]):
                    gather_y(t, y_rows[0:(B0[r] + RB[r]) * SLOTS, :])

        @block.scalar
        def _(act):
            act.dma_start(wqkv[:, :], wqkv_d).then_inc(wq_in, 16)
            act.dma_start(bqkv[:, :], bqkv_d.partition_broadcast(P)).then_inc(small_in[0], 16)
            act.dma_start(bproj[:, :], bproj_d.partition_broadcast(P)).then_inc(small_in[1], 16)
            act.dma_start(wproj[:, :], wproj_d).then_inc(small_in[2], 16)
            act.dma_start(wr[:, :], wr_d).then_inc(small_in[3], 16)
            act.dma_start(br[:, :], br_d.partition_broadcast(P)).then_inc(small_in[4], 16)
            act.dma_start(b1r[:, :], b1_d.rearrange("e (c p) -> (e c) p", p=P)).then_inc(small_in[5], 16)

            def copy_xT(u, par):
                act.wait_ge(xT_done, u + 1)
                nc.scalar.activation(xT_s[:, par, :], ps[:, par, 0:T], ACT.Copy).then_inc(xT_out, 1)

            copy_xT(0, 0)
            copy_xT(1, 1)

            def features(it, last):
                for par in range(2):
                    u = it * 2 + par
                    act.wait_ge(t_done, u + 1)
                    nc.scalar.activation(e_s[:, par], t_s[:, par], ACT.Relu, scale=-1.0).then_inc(relu_done, 1)
                    act.wait_ge(relu_done, u + 1)
                    nc.scalar.activation(e_s[:, par], e_s[:, par], ACT.Exp, scale=-1.0).then_inc(exp_done, 1)
                    if not last:
                        act.wait_ge(qkv_done, u + 1)
                        copy_xT(u + 2, par)

            with act.Fori(0, U // 2 - 1) as it:
                features(it, False)
            features(U // 2 - 1, True)

            act.wait_ge(b1T_done, 1)
            nc.scalar.activation(b1T[:, :], ps[:, 6, 0:E * HC], ACT.Copy).then_inc(b1T_out, 1)
            act.wait_ge(b1T_out, 1)

            def copy_yT(u, par):
                act.wait_ge(yT_done, u + 3)
                act.wait_ge(proj_done, u + 1)
                nc.scalar.activation(xT_s[:, par, :], ps[:, 6, 0:T], ACT.Copy).then_inc(yT_out, 1)

            with act.Fori(1, U // 4) as it:
                for par in range(2):
                    copy_yT(it * 2 + (par - 2), par)

            act.wait_ge(scale_done, 1)
            nc.scalar.activation(b1s[:], b1T[:], ACT.Copy, scale=sc[:, 17:18]).then_inc(achain, 1)
            with act.Fori(0, U // 4) as it:
                for par in range(2):
                    copy_yT(it * 2 + (U // 2 + par - 2), par)
                    e = it * 2 + par
                    w1e = wf[:, 0, bass.ds(e * HID, HID)]
                    w2e = wf2[:, bass.ds(e * HC, HC), :]
                    nc.scalar.activation(w1h[:, bass.ds(e, 1), :].rearrange("p a h -> p (a h)"), w1e, ACT.Copy,
                                         scale=sc[:, 12:13]).then_inc(whi_done, 1)
                    nc.scalar.activation(w2p[:, bass.ds(e * HC, HC), 0], w2e, ACT.Copy, scale=sc[:, 13:14]).then_inc(whi_done, 1)
            copy_yT(U - 2, 0)
            copy_yT(U - 1, 1)

            def split_high(it, par):
                u = it * 2 + par
                act.wait_ge(norm2_done, u + 1)
                nc.scalar.activation(tiles(x2row, u)[:, :, 0:D], xn_s[:, par], ACT.Copy, scale=X_SCALE).then_inc(xh_done, 1)

            def copy_x2T(u, par):
                act.wait_ge(x2T_done, u + 3)
                act.wait_ge(lg_done, u + 1)
                nc.scalar.activation(x2T[:, par], ps[:, 4 + par, :], ACT.Copy).then_inc(x2T_out, 1)

            split_high(0, 0)
            split_high(0, 1)
            copy_x2T(0, 0)

            def split_and_copy(it):
                split_high(it, 0)
                copy_x2T(it * 2 - 1, 1)
                split_high(it, 1)
                copy_x2T(it * 2, 0)

            with act.Fori(0, U // 4 - 1) as q:
                for k in range(2):
                    split_and_copy(q * 2 + (k + 1))
            split_and_copy(U // 2 - 1)
            copy_x2T(U - 1, 1)

            act.wait_ge(gap_done, 1)
            nc.scalar.activation(r1[:, 4, :], r1[:, 3, :], ACT.Exp).then_inc(gexp_done, 1)

            act.wait_ge(achain, 1)

            def copy_turned(n, j):
                act.wait_ge(turn_done, n + 3)
                act.wait_ge(up_done, n + 1)
                nc.scalar.activation(xgT[:, j % 2].rearrange("p w n -> p (w n)"), ps[:, j % 2, :], ACT.Copy).then_inc(turn_out, 1)

            def hidden_high(n, j):
                act.wait_ge(pre_done, n + 3)
                act.wait_ge(down_done, n + 1)
                nc.scalar.activation(hh[:, j % 2], pre[:, j % 2], ACT.Relu).then_inc(hi_done, 1)

            def copy_y_low(n, j):
                act.wait_ge(down_done, n + 3)
                act.wait_ge(y_sum_done, n + 1)
                nc.scalar.activation(y_low[:, j], ps[:, 6 + j, :].rearrange("p (g w d) -> p g w d", g=GPB, w=2)[:, :, 1],
                                     ACT.Copy).then_inc(y_low_done, 1)

            copy_turned(0, 0)
            copy_turned(1, 1)
            hidden_high(0, 0)
            copy_turned(2, 2)
            copy_turned(3, 3)

            def act_steps(it):
                for j in range(BODY):
                    n = it * BODY + j
                    if exists(n + 1):
                        hidden_high(n + 1, j + 1)
                    copy_y_low(n, j)
                    if exists(n + 4):
                        copy_turned(n + 4, j + 4)

            with act.Fori(0, ITERS - 2) as it:
                act_steps(it)
            act_steps(ITERS - 2)
            act_steps(ITERS - 1)

        @block.vector
        def _(dve):
            count = {"chain": 0}

            def link(ins):
                count["chain"] += 1
                ins.then_inc(chain, 1)
                dve.wait_ge(chain, count["chain"])

            for s, n in ((qkv_free, 4), (phi_done, 2), (pfx_done, 2 * TPU), (m_done, 2), (red_done, 2), (proj_done, 2), (lg_done, 2),
                         (x2_done, 1), (yT_done, 2), (yT_out, 1), (x2T_done, 2), (x2T_out, 2), (lgs_done, 2), (turn_done, 2), (turn_out, 2),
                         (up_done, 2), (pre_done, 2), (lo_done, 2), (down_done, 2), (y_sum_done, 2),
                         *((s, 16) for s in y_stored)):
                dve.sem_inc(s, n)

            def moments(t0, t1):
                me, qe, mo, qo = (st[:, t0:t1, c] for c in (1, 2, 4, 5))
                l = [lnt[:, c, t0:t1] for c in range(7)]
                nc.vector.tensor_tensor(l[0], me, mo, ALU.add)
                link(nc.vector.tensor_tensor(l[1], me, mo, ALU.subtract))
                nc.vector.tensor_tensor(l[2], qe, qo, ALU.add)
                link(nc.vector.scalar_tensor_tensor(out=l[5], in0=l[1], scalar=0.25, in1=l[1], op0=ALU.mult, op1=ALU.mult))
                nc.vector.tensor_scalar(l[3], l[0], 0.5, None, ALU.mult)
                link(nc.vector.scalar_tensor_tensor(out=l[6], in0=l[2], scalar=1.0 / D, in1=l[5], op0=ALU.mult, op1=ALU.add))
                return nc.vector.tensor_scalar(l[4], l[6], LN_EPS, None, ALU.add)

            def norm(u, par, which, done):
                for a in range(TPU):
                    t = u * TPU + a
                    ins = nc.vector.tensor_scalar(xn_s[:, par, a], x[:, bass.ds(t, 1), :].rearrange("p a d -> p (a d)"),
                                                  lnt[:, 3, bass.ds(t, 1)], rstd[:, which, bass.ds(t, 1)],
                                                  ALU.subtract, ALU.mult)
                ins.then_inc(done, 1)

            for g in range(LOADS):
                dve.wait_ge(x_in[g], 16)
                with dve.Fori(0, TPL // 4) as i:
                    for j in range(4):
                        t = i * 4 + (j + g * TPL)
                        nc.vector.bn_stats(st[:, bass.ds(t, 1), :].rearrange("p a s -> p (a s)"),
                                           x[:, bass.ds(t, 1), :].rearrange("p a d -> p (a d)")).then_inc(bn_done, 1)
                dve.wait_ge(bn_done, (g + 1) * TPL)
                moments(g * TPL, (g + 1) * TPL).then_inc(stats_done, 1)
                dve.wait_ge(stats_done, g + 1)
                if g == 1:
                    dve.wait_ge(rstd_done, 1)
                    norm(0, 0, 0, norm_done)
                    norm(1, 1, 0, norm_done)
            dve.wait_ge(rstd_done, LOADS)
            dve.wait_ge(small_in[0], 16)
            dve.wait_ge(const_done, 6)

            def project_in(it, last):
                for par in range(2):
                    u = it * 2 + par
                    pq = ps[:, 2 + 2 * par:4 + 2 * par, :]
                    dve.wait_ge(qkv_done, u + 1)
                    dve.wait_ge(phi_done, u + 1)
                    nc.vector.tensor_tensor(t_s[:, par], pq[:, :, 0:2 * D],
                                            bqkv[:, 0:2 * D].unsqueeze(1).broadcast_to([P, TPU, 2 * D]),
                                            ALU.add).then_inc(t_done, 1)
                    nc.vector.tensor_tensor(tiles(vaug, u)[:, :, :, 0:DH],
                                            pq[:, :, 2 * D:3 * D].rearrange("p a (h j) -> p a h j", j=DH),
                                            bqkv[:, 2 * D:3 * D].rearrange("p (h j) -> p h j", j=DH).unsqueeze(1)
                                            .broadcast_to([P, TPU, H, DH]), ALU.add).then_inc(qkv_free, 2)
                    if not last:
                        dve.wait_ge(xT_done, u + 1)
                        norm(u + 2, par, 0, norm_done)
                for par in range(2):
                    u = it * 2 + par
                    dve.wait_ge(exp_done, u + 1)
                    nc.vector.scalar_tensor_tensor(out=tiles(qk, u), in0=t_s[:, par], scalar=0.0, in1=e_s[:, par],
                                                   op0=ALU.max, op1=ALU.add).then_inc(phi_done, 1)

            with dve.Fori(0, U // 2 - 1) as it:
                project_in(it, False)
            project_in(U // 2 - 1, True)

            dve.wait_ge(w1_in, 16)
            dve.wait_ge(w2_in, 16)
            dve.wait_ge(b1T_out, 1)
            for n, w in enumerate((wf[:, 0], wf[:, 1], b1T[:, :])):
                nc.vector.tensor_reduce(sc[:, n:n + 1], w, AX.X, ALU.max, apply_absolute_value=True).then_inc(wmax_done, 1)


            def residual(u):
                dve.wait_ge(proj_done, u + 3)
                nc.vector.tensor_tensor(tiles(x, u), ps[:, 7, 0:T].rearrange("p (a d) -> p a d", a=TPU), tiles(x, u),
                                        ALU.add).then_inc(x2_done, 1)

            def statistics(u):
                dve.wait_ge(x2_done, u + 2)
                for a in range(TPU):
                    nc.vector.bn_stats(st[:, bass.ds(u * TPU + a, 1), :].rearrange("p a s -> p (a s)"),
                                       x[:, bass.ds(u * TPU + a, 1), :].rearrange("p a d -> p (a d)")).then_inc(bn_done, 1)

            def attend(it, first):
                for par in range(2):
                    u = it * 2 + par
                    for a in range(TPU):
                        t = u * TPU + a
                        dve.wait_ge(pfx_done, t + (2 * TPU + 1))
                        dve.wait_ge(red_done, t + 1)
                        q = qk[:, bass.ds(t, 1), 0:D].rearrange("p a (h i) -> p (a h) i", i=DH)
                        for g, (h0, h1) in enumerate(HEADS):
                            n = h1 - h0
                            ins = nc.vector.tensor_tensor(
                                m_s[:, a, h0 * KV:h1 * KV].rearrange("p (h j i) -> p h j i", j=DV, i=DH),
                                ps[:, 3 * a + g, 0:n * KV].rearrange("p (h j i) -> p h j i", j=DV, i=DH),
                                q[:, h0:h1, :].unsqueeze(2).broadcast_to([P, n, DV, DH]), ALU.mult)
                        ins.then_inc(m_done, 1)
                    if not first:
                        residual(u - 2)
                    for a in range(TPU):
                        t = u * TPU + a
                        dve.wait_ge(m_done, t + 3)
                        nc.vector.tensor_reduce(nd[:, bass.ds(t, 1), :].rearrange("p a n -> p (a n)"),
                                                m_s[:, a].rearrange("p (n i) -> p n i", i=DH), AX.X, ALU.add).then_inc(red_done, 1)
                    if not first:
                        statistics(u - 2)
                    dve.wait_ge(red_done, u * TPU + (TPU + 2))
                    dve.wait_ge(yT_done, u + 1)
                    nc.vector.tensor_scalar(rd[:, par], tiles(ndv, u)[:, :, :, DH], DEN_EPS, None, ALU.add).then_inc(den_done, 1)
                    dve.wait_ge(den_done, u + 1)
                    nc.vector.reciprocal(rd[:, par], rd[:, par]).then_inc(rd_done, 1)

            dve.wait_ge(xb_done, LOADS)
            dve.wait_ge(phi_done, U + 2)
            attend(0, True)
            with dve.Fori(1, U // 4) as it:
                attend(it, False)

            dve.wait_ge(wall_done, 1)
            i32 = lambda a, b: sc[:, a:b].bitcast(I32)
            EXPONENT = 0x7F800000
            link(nc.vector.tensor_scalar(sc[:, 8:10], sc[:, 4:6], 1e-18, None, ALU.max))
            link(nc.vector.tensor_scalar(i32(10, 12), i32(8, 10), EXPONENT, None, ALU.bitwise_and))
            link(nc.vector.scalar_tensor_tensor(out=sc[:, 14:15], in0=sc[:, 10:11], scalar=2.0 * D, in1=sc[:, 6:7],
                                                op0=ALU.mult, op1=ALU.add))
            link(nc.vector.tensor_scalar(i32(15, 16), i32(14, 15), EXPONENT, None, ALU.bitwise_and))
            link(nc.vector.reciprocal(sc[:, 16:17], sc[:, 15:16]))
            link(nc.vector.reciprocal(sc[:, 9:10], sc[:, 11:12]))
            link(nc.vector.tensor_scalar(sc[:, 13:14], sc[:, 9:10], W_TOP, None, ALU.mult))
            link(nc.vector.tensor_scalar(sc[:, 17:18], sc[:, 16:17], H_TOP, None, ALU.mult))
            link(nc.vector.tensor_scalar(sc[:, 12:13], sc[:, 17:18], 1.0 / X_SCALE, None, ALU.mult))
            link(nc.vector.tensor_tensor(sc[:, 19:20], sc[:, 17:18], sc[:, 13:14], ALU.mult))
            nc.vector.reciprocal(sc[:, 20:21], sc[:, 19:20]).then_inc(scale_done, 1)

            with dve.Fori(U // 4, 3 * U // 8) as it:
                attend(it, False)
            dve.wait_ge(bn_done, NT + NT // 2)
            moments(0, NT // 2).then_inc(var2_done, 1)
            with dve.Fori(3 * U // 8, U // 2) as it:
                attend(it, False)
            for u in (U - 2, U - 1):
                residual(u)
                statistics(u)
            dve.wait_ge(bn_done, 2 * NT)
            moments(NT // 2, NT).then_inc(var2_done, 1)
            dve.wait_ge(var2_done, 2)

            dve.wait_ge(small_in[6], 16)
            link(nc.vector.tensor_scalar(b2s, b2r, sc[0:E, 19:20], None, ALU.mult))
            link(nc.vector.tensor_copy(b2hml[:, 0], b2s))
            link(nc.vector.tensor_tensor(b2f, b2s, b2hml[:, 0], ALU.subtract))
            link(nc.vector.tensor_copy(b2hml[:, 1], b2f))
            nc.vector.tensor_tensor(b2hml[:, 2], b2f, b2hml[:, 1], ALU.subtract).then_inc(b2_done, 1)
            dve.wait_ge(b2_done, 1)

            dve.wait_ge(rstd_done, LOADS + 1)
            norm(0, 0, 1, norm2_done)
            norm(1, 1, 1, norm2_done)
            dve.wait_ge(rstd_done, LOADS + 2)
            dve.wait_ge(small_in[4], 16)

            def route(it, first, last):
                for par in range(2):
                    u = it * 2 + par
                    dve.wait_ge(xh_done, u + 1)
                    nc.vector.scalar_tensor_tensor(out=tiles(x2row, u)[:, :, D:2 * D], in0=xn_s[:, par], scalar=X_SCALE,
                                                   in1=tiles(x2row, u)[:, :, 0:D], op0=ALU.mult,
                                                   op1=ALU.subtract).then_inc(xl_done, 1)
                    if not last:
                        dve.wait_ge(xl_done, u + 1)
                        norm(u + 2, par, 1, norm2_done)
                if not first:
                    for par in range(2):
                        logits(it * 2 + (par - 2), par)

            def logits(u, par):
                dve.wait_ge(lg_done, u + 3)
                nc.vector.tensor_reduce(tiles(lg, u), ps[:, 6 + par, 0:TPU * 3 * E].rearrange("p (a w e) -> p a e w", a=TPU, w=3),
                                        AX.X, ALU.add).then_inc(lgs_done, 1)

            route(0, True, False)
            with dve.Fori(0, U // 4 - 1) as q:
                for k in range(2):
                    route(q * 2 + (k + 1), False, False)
            route(U // 2 - 1, False, True)
            logits(U - 2, 0)
            logits(U - 1, 1)
            dve.wait_ge(lgs_done, U + 2)
            link(nc.vector.scalar_tensor_tensor(out=lg[:, :, :], in0=lg[:, :, :], scalar=1.0 / X_SCALE,
                                                in1=br[:, :].unsqueeze(1).broadcast_to([P, NT, E]),
                                                op0=ALU.mult, op1=ALU.add))

            over_e = lambda a: a.unsqueeze(2).broadcast_to([P, NT, E])
            iota_t = iota[:, :].unsqueeze(1).broadcast_to([P, NT, E])

            def top(values, best, where, scratch, onehot):
                link(nc.vector.tensor_reduce(best, values, AX.X, ALU.max))
                link(nc.vector.tensor_tensor(scratch, values, over_e(best), ALU.is_equal))
                link(nc.vector.scalar_tensor_tensor(out=onehot, in0=iota_t, scalar=-float(E), in1=scratch,
                                                    op0=ALU.add, op1=ALU.mult))
                link(nc.vector.tensor_reduce(where, onehot, AX.X, ALU.min))
                link(nc.vector.scalar_tensor_tensor(out=onehot, in0=iota_t, scalar=-float(E), in1=over_e(where),
                                                    op0=ALU.add, op1=ALU.is_equal))

            top(lg[:, :, :], r1[:, 0, :], r1[:, 5, :], r8[:, 0], r8[:, 1])
            link(nc.vector.scalar_tensor_tensor(out=r8[:, 2], in0=r8[:, 1], scalar=-3.4e38, in1=lg[:, :, :],
                                                op0=ALU.mult, op1=ALU.add))
            top(r8[:, 2], r1[:, 1, :], r1[:, 6, :], r8[:, 0], r8[:, 3])
            nc.vector.tensor_tensor(r1[:, 3, :], r1[:, 1, :], r1[:, 0, :], ALU.subtract).then_inc(gap_done, 1)
            nc.vector.tensor_tensor(picked, r8[:, 1], r8[:, 3], ALU.add).then_inc(picked_done, 1)
            dve.wait_ge(gexp_done, 1)
            link(nc.vector.tensor_scalar(r1[:, 2, :], r1[:, 4, :], 1.0, None, ALU.add))
            link(nc.vector.reciprocal(r1[:, 7, :], r1[:, 2, :]))
            link(nc.vector.tensor_scalar(r1[:, 2, :], r1[:, 7, :], sc[:, 20:21], None, ALU.mult))
            link(nc.vector.tensor_tensor(r1[:, 7, :], r1[:, 2, :], r1[:, 4, :], ALU.mult))

            dve.wait_ge(count_done, 1)
            flat = lambda v: v.rearrange("p a b -> p (a b)")
            link(nc.vector.tensor_copy(tot, ps[:, 1, 0:NT * E].rearrange("p (t e) -> p e t", e=E)))
            dve.wait_ge(table_done, 15)
            link(nc.vector.tensor_tensor_scan(flat(upto), flat(in_round[:, :, :]), flat(tot), 0.0, ALU.mult, ALU.add))
            for r in range(R):
                nc.vector.tensor_copy(cnt[:, r, :], upto[:, :, T0[r] + RT[r] - 1]).then_inc(chain, 1)
            count["chain"] += R
            link(nc.vector.tensor_tensor(ahead, upto, tot, ALU.subtract))
            link(nc.vector.tensor_tensor(full, cnt.unsqueeze(3).broadcast_to([P, R, E, EXPERT_BLOCKS]),
                                         full_at[:, :].unsqueeze(1).unsqueeze(1).broadcast_to([P, R, E, EXPERT_BLOCKS]), ALU.is_gt))
            link(nc.vector.tensor_reduce(nblk, full, AX.X, ALU.add))
            link(nc.vector.tensor_tensor_scan(flat(ends), flat(in_row[:, :, :]), flat(nblk), 0.0, ALU.mult, ALU.add))
            link(nc.vector.tensor_tensor(base, ends, nblk, ALU.subtract))
            for r in range(R):
                link(nc.vector.tensor_scalar(base[:, r, :], base[:, r, :], float(SLOTS), float(B0[r] * SLOTS), ALU.mult, ALU.add))
            for r in range(R):
                rt = slice(T0[r], T0[r] + RT[r])
                link(nc.vector.tensor_tensor(ahead[:, :, rt], ahead[:, :, rt],
                                             base[:, r, :].unsqueeze(2).broadcast_to([P, E, RT[r]]), ALU.add))
            link(nc.vector.tensor_tensor(pos8, ps[:, 0, 0:NT * E].rearrange("p (t e) -> p t e", e=E),
                                         ahead.rearrange("p e t -> p t e"), ALU.add))
            for c, hot in enumerate((r8[:, 1], r8[:, 3])):
                link(nc.vector.tensor_tensor(r8[:, 0], hot, pos8, ALU.mult))
                link(nc.vector.tensor_reduce(pos_f[:, :, c], r8[:, 0], AX.X, ALU.add))
            link(nc.vector.tensor_copy(pos_i, pos_f))
            link(nc.vector.tensor_scalar(part_i[:, 0], pos_i, P - 1, None, ALU.bitwise_and))
            link(nc.vector.tensor_scalar(part_i[:, 1], pos_i, P.bit_length() - 1, None, ALU.logical_shift_right))
            nc.vector.tensor_copy(part_h, part_i).then_inc(part_done, 1)
            dve.wait_ge(part_done, 1)

            def slots(r):
                rt = slice(T0[r], T0[r] + RT[r])
                for c in range(TOP):
                    groups = slice(B0[r] * GPB, (B0[r] + RB[r]) * GPB)
                    nc.vector.tensor_tensor(group_eq[:, c, 0:RT[r], 0:RB[r] * GPB],
                                            group_of[:, groups].unsqueeze(1).broadcast_to([P, RT[r], RB[r] * GPB]),
                                            part_h[:, 1, rt, c].unsqueeze(2).broadcast_to([P, RT[r], RB[r] * GPB]),
                                            ALU.is_equal).then_inc(group_eq_done, 1)
                    nc.vector.tensor_tensor(slot_hot[:, c, rt, :], slot_of[:, :].unsqueeze(1).broadcast_to([P, RT[r], P]),
                                            part_h[:, 0, rt, c].unsqueeze(2).broadcast_to([P, RT[r], P]),
                                            ALU.is_equal).then_inc(slot_hot_done, 1)

            def tokens(r):
                dve.wait_ge(inverse_done, r + 1)
                nc.vector.tensor_scalar(ids[:, B0[r] * GPB:(B0[r] + RB[r]) * GPB], ps[:, 7, 0:RB[r] * GPB], float(MID), None,
                                        ALU.add).then_inc(ids_done, 1)

            slots(0)
            for r in range(R):
                past = slot_past[:, 0:RB[r] * E].rearrange("p (n e) -> p n e", e=E)
                link(nc.vector.tensor_tensor(past, ends[:, r, :].unsqueeze(1).broadcast_to([P, RB[r], E]),
                                             block_f[:, 0:RB[r]].unsqueeze(2).broadcast_to([P, RB[r], E]), ALU.is_le))
                link(nc.vector.tensor_reduce(expert_f[:, B0[r]:B0[r] + RB[r]], past, AX.X, ALU.add))
            expert_b = expert_f.rearrange("p (i j) -> p i j", j=BODY)
            link(nc.vector.tensor_scalar(expert_i[:, :, 0:BODY], expert_b, float(E - 1), None, ALU.min))
            nc.vector.memset(expert_i[:, ITERS - 1, BODY:], 0).then_inc(expert_done, 1)
            nc.vector.tensor_scalar(expert_i[:, 0:ITERS - 1, BODY:], expert_b[:, 1:ITERS, 0:2], float(E - 1), None,
                                    ALU.min).then_inc(expert_done, 1)
            tokens(0)
            slots(1)
            tokens(1)
            dve.wait_ge(expert_done, 2)
            dve_experts = expert_registers(dve, "dve")

            def hidden_pre(n, j):
                dve.wait_ge(up_done, n + 3)
                dve.wait_ge(lo_done, n + 1)
                e = expert(dve, dve_experts, j)
                bank = 2 + 2 * (j % 2)
                nc.vector.tensor_tensor(pre[:, j % 2], ps[:, bank:bank + 2, :].rearrange("p b (c n) -> p (b c) n", n=SLOTS),
                                        b1s[:, bass.ds(e * HC, HC)].unsqueeze(2).broadcast_to([P, HC, SLOTS]),
                                        ALU.add).then_inc(pre_done, 1)

            def hidden_low(n, j):
                dve.wait_ge(hi_done, n + 1)
                dve.wait_ge(down_done, n + 1)
                nc.vector.scalar_tensor_tensor(out=hl[:, j], in0=pre[:, j], scalar=0.0, in1=hh[:, j],
                                               op0=ALU.max, op1=ALU.subtract).then_inc(lo_done, 1)

            def sum_y(n, it, j):
                dve.wait_ge(y_low_done, n + 1)
                dve.wait_ge(y_stored[j], it * 16 + 16)
                nc.vector.tensor_tensor(ysb[:, j], ps[:, 6 + j, :].rearrange("p (g w d) -> p g w d", g=GPB, w=2)[:, :, 0],
                                        y_low[:, j], ALU.add).then_inc(y_sum_done, 1)

            def mix(t):
                dve.wait_ge(y_gathered[t % GATHERS], 16 * TOP * (t // GATHERS + 1))
                xt = x[:, t]
                nc.vector.scalar_tensor_tensor(out=xt, in0=yg[:, t, 0], scalar=r1[:, 2, t:t + 1], in1=xt,
                                               op0=ALU.mult, op1=ALU.add).then_inc(mix_half, 1)
                dve.wait_ge(mix_half, t + 1)
                nc.vector.scalar_tensor_tensor(out=xt, in0=yg[:, t, 1], scalar=r1[:, 7, t:t + 1], in1=xt,
                                               op0=ALU.mult, op1=ALU.add).then_inc(mix_done, 1)

            def dve_steps(it):
                load_experts(dve, dve_experts, it)
                for j in range(BODY):
                    n = it * BODY + j
                    if exists(n + 1):
                        hidden_pre(n + 1, j + 1)
                    hidden_low(n, j)
                    if j:
                        sum_y(n - 1, it, j - 1)
                    elif not isinstance(it, int) or it:
                        sum_y(n - 1, it - 1, BODY - 1)

            load_experts(dve, dve_experts, 0)
            hidden_pre(0, 0)
            dve_steps(0)
            with dve.Fori(1, ITERS - 1) as it:
                dve_steps(it)
            dve_steps(ITERS - 1)
            sum_y(NBLK - 1, ITERS - 1, BODY - 1)
            for t in range(NT):
                mix(t)

        @block.tensor
        def _(pe):
            pe.wait_ge(const_done, 6)

            def turn(bank, par, done):
                for a in range(TPU):
                    ins = nc.tensor.transpose(ps[:, bank, a * P:(a + 1) * P], xn_s[:, par, a], ident[:, :])
                ins.then_inc(done, 1)

            def turn_x(u, par):
                pe.wait_ge(norm_done, u + 1)
                turn(par, par, xT_done)

            turn_x(0, 0)
            turn_x(1, 1)
            pe.wait_ge(wq_in, 16)

            def qkv(it, last):
                for par in range(2):
                    u = it * 2 + par
                    pe.wait_ge(xT_out, u + 1)
                    pe.wait_ge(qkv_free, u * 2 + 2)
                    for a in range(TPU):
                        ins = nc.tensor.matmul(ps[:, 2 + 2 * par + a, 0:3 * D], xT_s[:, par, a * P:(a + 1) * P], wqkv[:, :],
                                               start=True, stop=True)
                    ins.then_inc(qkv_done, 1)
                if not last:
                    for par in range(2):
                        turn_x(it * 2 + par + 2, par)

            with pe.Fori(0, U // 2 - 1) as it:
                qkv(it, False)
            qkv(U // 2 - 1, True)

            pe.wait_ge(small_in[5], 16)
            nc.tensor.transpose(ps[:, 6, 0:E * HC], b1r[:, :], ident[0:E * HC, 0:E * HC]).then_inc(b1T_done, 1)

            pe.wait_ge(qkv_free, 2 * U + 4)

            def prefix(u, par, a):
                pe.wait_ge(kv_done, u * TPU + (a + 1))
                pe.wait_ge(m_done, u * TPU + (a + 1))
                for g, (h0, h1) in enumerate(HEADS):
                    o = ps[:, 3 * a + g, 0:(h1 - h0) * KV]
                    kv = [kv_s[:, par, b, h0:h1, :].rearrange("p h n -> p (h n)") for b in range(TPU)]
                    if a == 1:
                        nc.tensor.matmul(o, ones[:, :], kv[0], start=True, stop=False)
                    ins = nc.tensor.matmul(o, tri[:, :], kv[a], start=(a == 0), stop=True)
                ins.then_inc(pfx_done, 1)

            def turn_y(u, par):
                pe.wait_ge(y_done, u + 1)
                pe.wait_ge(yT_out, u + 1)
                turn(6, par, yT_done)

            def proj(u, par):
                pe.wait_ge(yT_out, u + 2)
                pe.wait_ge(x2_done, u + 1)
                for a in range(TPU):
                    ins = nc.tensor.matmul(ps[:, 7, a * P:(a + 1) * P], xT_s[:, par, a * P:(a + 1) * P], wproj[:, :],
                                           start=True, stop=True)
                ins.then_inc(proj_done, 1)

            for par in range(2):
                for a in range(TPU):
                    prefix(par, par, a)
            pe.wait_ge(b1T_out, 1)
            pe.wait_ge(small_in[2], 16)
            with pe.Fori(1, U // 2) as it:
                for par in range(2):
                    u = it * 2 + par
                    prefix(u, par, 0)
                    turn_y(u - 2, par)
                    prefix(u, par, 1)
                    proj(u - 2, par)
            for u in (U - 2, U - 1):
                turn_y(u, u % 2)
                proj(u, u % 2)

            pe.wait_ge(table_done, 15)
            pe.wait_ge(wr_done, 4)

            def router(it):
                for par in range(2):
                    u = it * 2 + par
                    pe.wait_ge(xl_done, u + 1)
                    pe.wait_ge(x2T_out, u + 1)
                    for w in range(2):
                        for a in range(TPU):
                            at = (w * TPU + a) * P
                            rows = x2row[:, bass.ds(u * TPU + a, 1), w * D:(w + 1) * D].rearrange("p a d -> p (a d)")
                            ins = nc.tensor.matmul(ps[:, 4 + par, at:at + P], rows, ident_h[:, :], start=True, stop=True)
                    ins.then_inc(x2T_done, 1)
                for par in range(2):
                    u = it * 2 + par
                    pe.wait_ge(x2T_out, u + 3)
                    pe.wait_ge(lgs_done, u + 1)
                    for a in range(TPU):
                        for w in range(2):
                            at = (w * TPU + a) * P
                            ins = nc.tensor.matmul(ps[:, 6 + par, a * 3 * E:(a + 1) * 3 * E], x2T[:, par, at:at + P],
                                                   wr_parts[:, :, :].rearrange("p w e -> p (w e)"), start=(w == 0), stop=(w == 1))
                    ins.then_inc(lg_done, 1)

            with pe.Fori(0, U // 4) as q:
                for k in range(2):
                    router(q * 2 + k)

            pe.wait_ge(table_done, 15)
            pe.wait_ge(picked_done, 1)
            nc.tensor.matmul(ps[:, 0, 0:NT * E], before_h[:, :], picked.rearrange("p t e -> p (t e)"), start=True, stop=True)
            nc.tensor.matmul(ps[:, 1, 0:NT * E], ones_h[:, :], picked.rearrange("p t e -> p (t e)"),
                             start=True, stop=True).then_inc(count_done, 1)

            for r in range(R):
                if r:
                    pe.wait_ge(ids_done, r)
                for c in range(TOP):
                    pe.wait_ge(slot_hot_done, r * TOP + (c + 1))
                    pe.wait_ge(group_hot_done, r * TOP + (c + 1))
                    for t in range(T0[r], T0[r] + RT[r]):
                        first, last = t == T0[r] and c == 0, t == T0[r] + RT[r] - 1 and c == TOP - 1
                        ins = nc.tensor.matmul(ps[:, 7, 0:RB[r] * GPB], slot_hot[:, c, t, :], group_hot[:, c, t, 0:RB[r] * GPB],
                                               start=first, stop=last)
                ins.then_inc(inverse_done, 1)

            pe.wait_ge(wlo_done, 2)
            pe.wait_ge(b2_in, 32)
            pe.wait_ge(expert_done, 2)
            pe_experts = expert_registers(pe, "pe", PE_PASSES)

            def turn_block(it, j):
                pe.wait_ge(gathered[j % 2], (it + j // BODY) * (16 * GPB) + 16 * GPB)
                pe.wait_ge(turn_out, it * BODY + (j + 1))
                rows = xg[:, bass.ds(it * BODY + j, 1)]
                for g in range(GPB):
                    for w in range(2):
                        at = w * SLOTS + g * P
                        ins = nc.tensor.matmul(ps[:, j % 2, at:at + P], rows[:, :, g, w].rearrange("p a d -> p (a d)"), ident_h[:, :],
                                               start=True, stop=True)
                ins.then_inc(turn_done, 1)

            def up(n, j, k=0):
                e = expert(pe, pe_experts, k * (BODY + 2) + j)
                pe.wait_ge(turn_out, n + 3)
                pe.wait_ge(pre_done, n + 1)
                xh, xl = xgT[:, j % 2, 0], xgT[:, j % 2, 1]
                for c in range(HC):
                    col = c % 2 * SLOTS
                    o = ps[:, 2 + 2 * (j % 2) + c // 2, col:col + SLOTS]
                    wh, wl = (w[:, bass.ds(e, 1), c * P:(c + 1) * P].rearrange("p a h -> p (a h)") for w in (w1h, w1l))
                    nc.tensor.matmul(o, wh, xh, start=True, stop=False)
                    nc.tensor.matmul(o, wh, xl, start=False, stop=False)
                    ins = nc.tensor.matmul(o, wl, xh, start=False, stop=True)
                ins.then_inc(up_done, 1)

            def down(n, j, k):
                e = expert(pe, pe_experts, k * (BODY + 2) + j)
                pe.wait_ge(y_sum_done, n + 1)
                pe.wait_ge(lo_done, n + 3)
                rows = [ps[:, 6 + j, g * 2 * D:(g + 1) * 2 * D] for g in range(GPB)]
                for c in range(HC):
                    wc = w2[:, bass.ds(e, 1), c].rearrange("p a w d -> p (a w d)")
                    wh = w2[:, bass.ds(e, 1), c, 0].rearrange("p a d -> p (a d)")
                    for g, o in enumerate(rows):
                        slots_g = slice(g * P, (g + 1) * P)
                        nc.tensor.matmul(o, hh[:, j, c, slots_g], wc, start=(c == 0 and g == 0), stop=False)
                        nc.tensor.matmul(o[:, 0:D], hl[:, j, c, slots_g], wh, start=False, stop=False)
                for g, o in enumerate(rows):
                    ins = nc.tensor.matmul(o[:, 0:D], ones3[:, :], b2p[:, bass.ds(e, 1), :].rearrange("p a d -> p (a d)"),
                                           start=False, stop=(g == GPB - 1))
                ins.then_inc(down_done, 1)

            def pe_steps(it, k):
                for j in range(BODY):
                    n = it * BODY + j
                    if exists(n + 2):
                        up(n + 2, j + 2, k)
                    down(n, j, k)
                    if exists(n + 4):
                        turn_block(it, j + 4)

            load_experts(pe, pe_experts[0:BODY + 2], 0)
            turn_block(0, 0)
            turn_block(0, 1)
            up(0, 0)
            turn_block(0, 2)
            up(1, 1)
            turn_block(0, 3)
            with pe.Fori(0, (ITERS - 2) // PE_PASSES) as q:
                load_experts(pe, pe_experts, q * PE_PASSES)
                for k in range(PE_PASSES):
                    pe_steps(q * PE_PASSES + k, k)
            load_experts(pe, pe_experts[0:2 * (BODY + 2)], ITERS - 2)
            pe_steps(ITERS - 2, 0)
            pe_steps(ITERS - 1, 1)



_INS = ['L0_attn_x', 'L0_attn_W_attn', 'L0_attn_b_attn', 'L0_attn_W_proj', 'L0_attn_b_proj', 'L0_ffn_W1', 'L0_ffn_b1',
        'L0_ffn_W2', 'L0_ffn_b2', 'L0_ffn_Wr', 'L0_ffn_br']


def kernel(**inputs):
    import numpy as _np
    import concourse.bacc as _bacc
    from concourse import mybir as _mybir
    from concourse.bass_utils import run_bass_kernel_spmd as _run

    nc = _bacc.Bacc("TRN2", target_bir_lowering=False, num_devices=1)
    arrays, args = {}, []
    for name in _INS:
        a = _np.ascontiguousarray(inputs[name])
        arrays[f"in_{name}_dram"] = a
        args.append(nc.dram_tensor(f"in_{name}_dram", a.shape, _mybir.dt.from_np(a.dtype), kind="ExternalInput").ap())
    out = nc.dram_tensor("out_dram", inputs['L0_attn_x'].shape, F32, kind="ExternalOutput").ap()
    block_kernel(nc, *args, out)
    r = _run(nc, [arrays], core_ids=[0])
    return r.results[0]["out_dram"]
```
